# Optimizing a Trainium2 kernel written in Bass

```python
import numpy as np
import jax
import jax.numpy as jnp

def _softmax(x, axis=-1):
    return jax.nn.softmax(x, axis=axis)

def _gelu(x):
    return jax.nn.gelu(x, approximate=True)

def _silu(x):
    return jax.nn.silu(x)

def _sigmoid(x):
    return jax.nn.sigmoid(x)

def _layernorm(x, axis=-1, eps=1e-05):
    m = jnp.mean(x, axis=axis, keepdims=True)
    v = jnp.var(x, axis=axis, keepdims=True)
    return (x - m) / jnp.sqrt(v + eps)

def _scatter_add(tgt, idx, src, axis=0):
    return tgt.at[idx].add(src)

def _segment_sum(src, seg, n):
    return jax.ops.segment_sum(src, seg, n)
kernel_name = 'mk_macaron_d4_jaxref_r8_67c879'

def setup_inputs(seed: int=0):
    np.random.seed(seed)
    _w = jnp.asarray

    def _L0_attn_setup():
        import jax, jax.numpy as jnp
        import numpy as np
        N_EMBD = 128
        N_HEAD = 16
        HEAD_DIM = N_EMBD // N_HEAD
        LATENT_DIM = N_EMBD // 2
        B, T = (4, 256)
        key = jax.random.key(seed)
        ks = jax.random.split(key, 5)

        def init(k, fan_in, fan_out):
            bound = 1.0 / np.sqrt(fan_in)
            return jax.random.uniform(k, (fan_in, fan_out), jnp.float32, -bound, bound)
        return {'x': jax.random.normal(ks[0], (B, T, N_EMBD), jnp.float32), 'Wc_down': init(ks[1], N_EMBD, LATENT_DIM), 'Wq_up': init(ks[2], LATENT_DIM, N_EMBD), 'Wkv_up': init(ks[3], LATENT_DIM, 2 * HEAD_DIM), 'Wc_proj': init(ks[4], N_EMBD, N_EMBD)}
    _L0_attn_in = _L0_attn_setup()

    def _L0_ffn_setup():
        import jax, jax.numpy as jnp
        import numpy as np
        IN_DIM = 128
        OUT_DIM = 128
        NUM_EXPERTS = 8
        TOP_K = 2
        key = jax.random.key(seed)
        ks = jax.random.split(key, 5)
        s = 1.0 / np.sqrt(IN_DIM)
        x = jax.random.normal(ks[0], (4, 256, IN_DIM), dtype=jnp.float32)
        Wg = jax.random.uniform(ks[1], (IN_DIM, NUM_EXPERTS), jnp.float32, -s, s)
        bg = jnp.zeros((NUM_EXPERTS,), jnp.float32)
        We = jax.random.uniform(ks[2], (NUM_EXPERTS, OUT_DIM, IN_DIM), jnp.float32, -s, s)
        be = jax.random.uniform(ks[3], (NUM_EXPERTS, OUT_DIM), jnp.float32, -s, s)
        return {'x': x, 'Wg': Wg, 'bg': bg, 'We': We, 'be': be}
    _L0_ffn_in = _L0_ffn_setup()

    def _L1_attn_setup():
        import jax, jax.numpy as jnp
        import numpy as np
        HIDDEN = 128
        HEADS = 16
        HEAD_DIM = HIDDEN // HEADS
        ROPE_BASE = 10000.0

        def _rope_cos_sin(seq_len, dim):
            inv_freq = 1.0 / ROPE_BASE ** (jnp.arange(0, dim, 2, dtype=jnp.float32) / dim)
            t = jnp.arange(seq_len, dtype=jnp.float32)
            freqs = jnp.einsum('i,j->ij', t, inv_freq)
            emb = jnp.concatenate([freqs, freqs], axis=-1)
            return (jnp.cos(emb), jnp.sin(emb))

        def _apply_rope(x, cos, sin):
            x1, x2 = (x[..., 0::2], x[..., 1::2])
            c = cos[..., :x1.shape[-1]]
            s = sin[..., :x1.shape[-1]]
            return jnp.concatenate([x1 * c - x2 * s, x1 * s + x2 * c], axis=-1)
        key = jax.random.key(seed)
        ks = jax.random.split(key, 9)
        B, S = (4, 256)
        lim = 1.0 / np.sqrt(HIDDEN)

        def lin(kw, kb):
            W = jax.random.uniform(kw, (HIDDEN, HIDDEN), jnp.float32, -lim, lim)
            b = jax.random.uniform(kb, (HIDDEN,), jnp.float32, -lim, lim)
            return (W, b)
        Wq, bq = lin(ks[0], ks[1])
        Wk, bk = lin(ks[2], ks[3])
        Wv, bv = lin(ks[4], ks[5])
        Wo, bo = lin(ks[6], ks[7])
        x = jax.random.normal(ks[8], (B, S, HIDDEN), jnp.float32)
        return {'x': x, 'Wq': Wq, 'bq': bq, 'Wk': Wk, 'bk': bk, 'Wv': Wv, 'bv': bv, 'Wo': Wo, 'bo': bo}
    _L1_attn_in = _L1_attn_setup()

    def _L1_ffn_setup():
        import jax, jax.numpy as jnp
        import numpy as np
        DIM = 128

        def _reference_tuple_inner(x, W_r, W_k, W_v, mu_r, mu_k):
            B, T, C = x.shape
            x_prev = jnp.concatenate([jnp.zeros((B, 1, C), x.dtype), x[:, :-1, :]], axis=1)
            xr = mu_r * x + (1.0 - mu_r) * x_prev
            xk = mu_k * x + (1.0 - mu_k) * x_prev
            r = jax.nn.sigmoid(jnp.einsum('btc,dc->btd', xr, W_r))
            k = jnp.einsum('btc,dc->btd', xk, W_k)
            k_act = jnp.square(jax.nn.relu(k))
            out = r * jnp.einsum('btc,dc->btd', k_act, W_v)
            new_state = x[:, -1, :]
            return (out, new_state)
        key = jax.random.key(seed)
        ks = jax.random.split(key, 6)
        B, T, C = (8, 256, DIM)
        x = jax.random.normal(ks[0], (B, T, C), dtype=jnp.float32)
        s = 1.0 / np.sqrt(C)
        W_r = jax.random.uniform(ks[1], (C, C), jnp.float32, -s, s)
        W_k = jax.random.uniform(ks[2], (C, C), jnp.float32, -s, s)
        W_v = jax.random.uniform(ks[3], (C, C), jnp.float32, -s, s)
        mu_r = jax.random.uniform(ks[4], (C,), jnp.float32)
        mu_k = jax.random.uniform(ks[5], (C,), jnp.float32)
        return {'x': x, 'W_r': W_r, 'W_k': W_k, 'W_v': W_v, 'mu_r': mu_r, 'mu_k': mu_k}
    _L1_ffn_in = _L1_ffn_setup()

    def _L2_attn_setup():
        import jax, jax.numpy as jnp
        import numpy as np
        S_LEN, BATCH, HID, HEADS = (256, 4, 128, 16)
        HD = HID // HEADS

        def _forget_attention(hidden_states, Wq, bq, Wk, bk, Wv, bv, Wf, bf, Wo, bo):
            S, B, H = hidden_states.shape
            nh, hd = (HEADS, HD)

            def shape(x):
                return x.reshape(S, B, nh, hd)
            q = shape(hidden_states @ Wq.T + bq)
            k = shape(hidden_states @ Wk.T + bk)
            v = shape(hidden_states @ Wv.T + bv)
            phi_q = jax.nn.elu(q) + 1.0
            phi_k = jax.nn.elu(k) + 1.0
            f = jax.nn.sigmoid(hidden_states @ Wf.T + bf)

            def step(carry, xs):
                Sm, z = carry
                ft, pk, pq, vt = xs
                fte = ft[..., None]
                Sm = fte[..., None] * Sm + pk[..., :, None] * vt[..., None, :]
                z = fte * z + pk
                num = jnp.einsum('bhd,bhde->bhe', pq, Sm)
                den = jnp.einsum('bhd,bhd->bh', pq, z)[..., None]
                return ((Sm, z), num / (den + 1e-06))
            init = (jnp.zeros((B, nh, hd, hd), hidden_states.dtype), jnp.zeros((B, nh, hd), hidden_states.dtype))
            _, out = jax.lax.scan(step, init, (f, phi_k, phi_q, v))
            out = out.reshape(S, B, H) @ Wo.T + bo
            return (out, f)

        def _reference_tuple_inner(hidden_states, Wq, bq, Wk, bk, Wv, bv, Wf, bf, Wo, bo):
            out, f = _forget_attention(hidden_states, Wq, bq, Wk, bk, Wv, bv, Wf, bf, Wo, bo)
            return (out, jnp.zeros_like(out), f)
        key = jax.random.key(seed)
        ks = jax.random.split(key, 6)

        def lin_w(k, out_dim, in_dim):
            return jax.random.normal(k, (out_dim, in_dim), jnp.float32) * (1.0 / np.sqrt(in_dim))
        return {'hidden_states': jax.random.normal(ks[0], (S_LEN, BATCH, HID), jnp.float32), 'Wq': lin_w(ks[1], HID, HID), 'bq': jnp.zeros((HID,), jnp.float32), 'Wk': lin_w(ks[2], HID, HID), 'bk': jnp.zeros((HID,), jnp.float32), 'Wv': lin_w(ks[3], HID, HID), 'bv': jnp.zeros((HID,), jnp.float32), 'Wf': lin_w(ks[4], HEADS, HID), 'bf': jnp.zeros((HEADS,), jnp.float32), 'Wo': lin_w(ks[5], HID, HID), 'bo': jnp.zeros((HID,), jnp.float32)}
    _L2_attn_in = _L2_attn_setup()

    def _L2_ffn_setup():
        import jax, jax.numpy as jnp
        import numpy as np
        DIM = 128
        HIDDEN = 384
        SCALE = 1.0 / 127.0

        def _dequant(w_int, dtype):
            return w_int.astype(dtype) * jnp.asarray(SCALE, dtype)
        key = jax.random.key(seed)
        k_x, k_g, k_u, k_d = jax.random.split(key, 4)
        x = jax.random.normal(k_x, (4, 256, DIM), dtype=jnp.float32)
        w_gate = jax.random.randint(k_g, (HIDDEN, DIM), -127, 128, dtype=jnp.int32)
        w_up = jax.random.randint(k_u, (HIDDEN, DIM), -127, 128, dtype=jnp.int32)
        w_down = jax.random.randint(k_d, (DIM, HIDDEN), -127, 128, dtype=jnp.int32)
        return {'x': x, 'w_gate': w_gate, 'w_up': w_up, 'w_down': w_down}
    _L2_ffn_in = _L2_ffn_setup()

    def _L3_attn_setup():
        import jax, jax.numpy as jnp
        import numpy as np
        import math
        B, T, C, D = (8, 256, 128, 128)
        N_LAYER, LAYER_ID = (24, 12)

        def _wkv(time_decay, time_first, k, v):
            ew = jnp.exp(-jnp.exp(time_decay))
            eu = jnp.exp(time_first)
            ek = jnp.exp(k)
            ekv = ek * v

            def step(carry, inp):
                a, b = carry
                ekt, ekvt = inp
                out = (eu * ekvt + a) / (eu * ekt + b)
                return ((ew * a + ekvt, ew * b + ekt), out)
            init = (jnp.zeros_like(ek[:, 0]), jnp.zeros_like(ek[:, 0]))
            xs = (jnp.swapaxes(ek, 0, 1), jnp.swapaxes(ekv, 0, 1))
            _, out = jax.lax.scan(step, init, xs)
            return jnp.swapaxes(out, 0, 1)
        key = jax.random.key(seed)
        ks = jax.random.split(key, 5)
        r01 = LAYER_ID / (N_LAYER - 1)
        r10 = 1.0 - LAYER_ID / N_LAYER
        ddd = np.arange(C, dtype=np.float64) / C
        h = np.arange(D, dtype=np.float64)
        decay_speed = -5 + 8 * (h / (D - 1)) ** (0.7 + 1.3 * r01)
        zigzag = ((np.arange(D) + 1) % 3 - 1) * 0.5
        time_first = np.log(0.3) + zigzag
        scale = C ** (-0.5)
        return {'x': jax.random.normal(ks[0], (B, T, C), jnp.float32), 'time_decay': jnp.asarray(decay_speed, jnp.float32), 'time_first': jnp.asarray(time_first, jnp.float32), 'time_mix_k': jnp.asarray(ddd ** r10, jnp.float32), 'time_mix_v': jnp.asarray(ddd ** r10 + 0.3 * r01, jnp.float32), 'time_mix_r': jnp.asarray(ddd ** (0.5 * r10), jnp.float32), 'Wk': jax.random.normal(ks[1], (D, C), jnp.float32) * scale, 'Wv': jax.random.normal(ks[2], (D, C), jnp.float32) * scale, 'Wr': jax.random.normal(ks[3], (D, C), jnp.float32) * scale, 'Wo': jax.random.normal(ks[4], (C, D), jnp.float32) * scale}
    _L3_attn_in = _L3_attn_setup()

    def _L3_ffn_setup():
        import jax, jax.numpy as jnp
        import numpy as np
        DIM = 128
        DEPTH = 6
        HEADS = 16
        DIM_HEAD = 64
        WINDOW = 32
        INNER = HEADS * DIM_HEAD
        DIM_INNER = int(DIM * 4 * 2 / 3)
        QK_SCALE = 8.0

        def shift_tokens(t):
            a, s = jnp.split(t, 2, -1)
            s = jnp.pad(s, ((0, 0), (1, 0), (0, 0)))[:, :-1]
            return jnp.concatenate([a, s], -1)

        def l2norm(t):
            return t / jnp.maximum(jnp.linalg.norm(t, axis=-1, keepdims=True), 1e-12)

        def rotate_half(x):
            x1, x2 = jnp.split(x, 2, -1)
            return jnp.concatenate([-x2, x1], -1)

        def rotary_tables(n):
            half = jnp.arange(0, DIM_HEAD, 2, dtype=jnp.float32)
            inv_freq = 1.0 / 10000.0 ** (half / DIM_HEAD)
            t = jnp.arange(n, dtype=jnp.float32)
            freqs = t[:, None] * inv_freq[None, :]
            freqs = jnp.concatenate([freqs, freqs], -1)
            base_scale = (half + 0.4 * DIM_HEAD) / (1.4 * DIM_HEAD)
            power = (t - n // 2) / (WINDOW // 2)
            scale = base_scale[None, :] ** power[:, None]
            scale = jnp.concatenate([scale, scale], -1)
            return (freqs, scale)

        def local_attention(q, k, v):
            b, h, n, d = q.shape
            w = WINDOW
            nw = n // w
            bq = q.reshape(b, h, nw, w, d)
            bk = k.reshape(b, h, nw, w, d)
            bv = v.reshape(b, h, nw, w, d)

            def look(t):
                p = jnp.pad(t, ((0, 0), (0, 0), (1, 0), (0, 0), (0, 0)))
                return jnp.concatenate([p[:, :, :nw], p[:, :, 1:]], axis=3)
            bk2, bv2 = (look(bk), look(bv))
            seq = jnp.arange(n).reshape(nw, w)
            seq_p = jnp.pad(seq, ((1, 0), (0, 0)), constant_values=-1)
            jt = jnp.concatenate([seq_p[:nw], seq_p[1:]], axis=1)
            it = seq[:, :, None]
            jb = jt[:, None, :]
            mask = (it < jb) | (it > jb + w) | (jb == -1)
            sim = jnp.einsum('bhwie,bhwje->bhwij', bq, bk2) * QK_SCALE
            sim = jnp.where(mask, -jnp.finfo(sim.dtype).max, sim)
            attn = jax.nn.softmax(sim, -1)
            out = jnp.einsum('bhwij,bhwje->bhwie', attn, bv2)
            return out.reshape(b, h, n, d)

        def attn_layer(x, Wqkv, qs, ksc, Wo):
            b, n, _ = x.shape
            qkv = x @ Wqkv
            q, k, v = jnp.split(qkv, 3, -1)
            sh = lambda t: t.reshape(b, n, HEADS, DIM_HEAD).transpose(0, 2, 1, 3)
            q, k, v = (sh(q), sh(k), sh(v))
            q = l2norm(q) * qs
            k = l2norm(k) * ksc
            freqs, scale = rotary_tables(n)
            cos, sin = (jnp.cos(freqs), jnp.sin(freqs))
            q = q * cos * scale + rotate_half(q) * sin * scale
            inv = 1.0 / scale
            k = k * cos * inv + rotate_half(k) * sin * inv
            out = local_attention(q, k, v)
            out = out.transpose(0, 2, 1, 3).reshape(b, n, INNER)
            return out @ Wo

        def ffn_layer(x, g, bln, W1, b1, W2, b2):
            mu = x.mean(-1, keepdims=True)
            var = ((x - mu) ** 2).mean(-1, keepdims=True)
            xn = (x - mu) / jnp.sqrt(var + 1e-05) * g + bln
            hg = xn @ W1 + b1
            a, gate = jnp.split(hg, 2, -1)
            return a * jax.nn.gelu(gate, approximate=False) @ W2 + b2
        key = jax.random.key(seed)
        ks = jax.random.split(key, 8)
        B, N = (2, 256)
        init = lambda k, shape: jax.random.normal(k, shape, jnp.float32) * 0.02
        return {'x': jax.random.normal(ks[0], (B, N, DIM), jnp.float32), 'Wqkv': init(ks[1], (DEPTH, DIM, 3 * INNER)), 'q_scale': jnp.ones((DEPTH, DIM_HEAD), jnp.float32), 'k_scale': jnp.ones((DEPTH, DIM_HEAD), jnp.float32), 'Wo': init(ks[2], (DEPTH, INNER, DIM)), 'ln_g': jnp.ones((DEPTH, DIM), jnp.float32), 'ln_b': jnp.zeros((DEPTH, DIM), jnp.float32), 'W1': init(ks[3], (DEPTH, DIM, 2 * DIM_INNER)), 'b1': jnp.zeros((DEPTH, 2 * DIM_INNER), jnp.float32), 'W2': init(ks[4], (DEPTH, DIM_INNER, DIM)), 'b2': jnp.zeros((DEPTH, DIM), jnp.float32)}
    _L3_ffn_in = _L3_ffn_setup()
    _d = {'L0_attn_x': _L0_attn_in['x'], 'L0_attn_Wc_down': _L0_attn_in['Wc_down'], 'L0_attn_Wq_up': _L0_attn_in['Wq_up'], 'L0_attn_Wkv_up': _L0_attn_in['Wkv_up'], 'L0_attn_Wc_proj': _L0_attn_in['Wc_proj'], 'L0_ffn_Wg': _L0_ffn_in['Wg'], 'L0_ffn_bg': _L0_ffn_in['bg'], 'L0_ffn_We': _L0_ffn_in['We'], 'L0_ffn_be': _L0_ffn_in['be'], 'L1_attn_Wq': _L1_attn_in['Wq'], 'L1_attn_bq': _L1_attn_in['bq'], 'L1_attn_Wk': _L1_attn_in['Wk'], 'L1_attn_bk': _L1_attn_in['bk'], 'L1_attn_Wv': _L1_attn_in['Wv'], 'L1_attn_bv': _L1_attn_in['bv'], 'L1_attn_Wo': _L1_attn_in['Wo'], 'L1_attn_bo': _L1_attn_in['bo'], 'L1_ffn_W_r': _L1_ffn_in['W_r'], 'L1_ffn_W_k': _L1_ffn_in['W_k'], 'L1_ffn_W_v': _L1_ffn_in['W_v'], 'L1_ffn_mu_r': _L1_ffn_in['mu_r'], 'L1_ffn_mu_k': _L1_ffn_in['mu_k'], 'L2_attn_Wq': _L2_attn_in['Wq'], 'L2_attn_bq': _L2_attn_in['bq'], 'L2_attn_Wk': _L2_attn_in['Wk'], 'L2_attn_bk': _L2_attn_in['bk'], 'L2_attn_Wv': _L2_attn_in['Wv'], 'L2_attn_bv': _L2_attn_in['bv'], 'L2_attn_Wf': _L2_attn_in['Wf'], 'L2_attn_bf': _L2_attn_in['bf'], 'L2_attn_Wo': _L2_attn_in['Wo'], 'L2_attn_bo': _L2_attn_in['bo'], 'L2_ffn_w_gate': _L2_ffn_in['w_gate'], 'L2_ffn_w_up': _L2_ffn_in['w_up'], 'L2_ffn_w_down': _L2_ffn_in['w_down'], 'L3_attn_time_decay': _L3_attn_in['time_decay'], 'L3_attn_time_first': _L3_attn_in['time_first'], 'L3_attn_time_mix_k': _L3_attn_in['time_mix_k'], 'L3_attn_time_mix_v': _L3_attn_in['time_mix_v'], 'L3_attn_time_mix_r': _L3_attn_in['time_mix_r'], 'L3_attn_Wk': _L3_attn_in['Wk'], 'L3_attn_Wv': _L3_attn_in['Wv'], 'L3_attn_Wr': _L3_attn_in['Wr'], 'L3_attn_Wo': _L3_attn_in['Wo'], 'L3_ffn_Wqkv': _L3_ffn_in['Wqkv'], 'L3_ffn_q_scale': _L3_ffn_in['q_scale'], 'L3_ffn_k_scale': _L3_ffn_in['k_scale'], 'L3_ffn_Wo': _L3_ffn_in['Wo'], 'L3_ffn_ln_g': _L3_ffn_in['ln_g'], 'L3_ffn_ln_b': _L3_ffn_in['ln_b'], 'L3_ffn_W1': _L3_ffn_in['W1'], 'L3_ffn_b1': _L3_ffn_in['b1'], 'L3_ffn_W2': _L3_ffn_in['W2'], 'L3_ffn_b2': _L3_ffn_in['b2']}
    _x0 = _d['L0_attn_x']
    _d['L0_attn_x'] = jax.random.normal(jax.random.fold_in(jax.random.key(seed), 1), (4, 512, 128), dtype=_x0.dtype)
    del _x0
    return _d

def reference(L0_attn_x, L0_attn_Wc_down, L0_attn_Wq_up, L0_attn_Wkv_up, L0_attn_Wc_proj, L0_ffn_Wg, L0_ffn_bg, L0_ffn_We, L0_ffn_be, L1_attn_Wq, L1_attn_bq, L1_attn_Wk, L1_attn_bk, L1_attn_Wv, L1_attn_bv, L1_attn_Wo, L1_attn_bo, L1_ffn_W_r, L1_ffn_W_k, L1_ffn_W_v, L1_ffn_mu_r, L1_ffn_mu_k, L2_attn_Wq, L2_attn_bq, L2_attn_Wk, L2_attn_bk, L2_attn_Wv, L2_attn_bv, L2_attn_Wf, L2_attn_bf, L2_attn_Wo, L2_attn_bo, L2_ffn_w_gate, L2_ffn_w_up, L2_ffn_w_down, L3_attn_time_decay, L3_attn_time_first, L3_attn_time_mix_k, L3_attn_time_mix_v, L3_attn_time_mix_r, L3_attn_Wk, L3_attn_Wv, L3_attn_Wr, L3_attn_Wo, L3_ffn_Wqkv, L3_ffn_q_scale, L3_ffn_k_scale, L3_ffn_Wo, L3_ffn_ln_g, L3_ffn_ln_b, L3_ffn_W1, L3_ffn_b1, L3_ffn_W2, L3_ffn_b2):

    def _L0_attn_ref(x, Wc_down, Wq_up, Wkv_up, Wc_proj):
        import jax, jax.numpy as jnp
        import numpy as np
        N_EMBD = 128
        N_HEAD = 16
        HEAD_DIM = N_EMBD // N_HEAD
        LATENT_DIM = N_EMBD // 2
        B, T = (4, 256)
        Bsz, Tlen, C = x.shape
        latent = x @ Wc_down
        q = (latent @ Wq_up).reshape(Bsz, Tlen, N_HEAD, HEAD_DIM)
        kv = latent @ Wkv_up
        k, v = (kv[..., :HEAD_DIM], kv[..., HEAD_DIM:])
        scale = 1.0 / np.sqrt(HEAD_DIM)
        att = jnp.einsum('bthd,bsd->bhts', q, k) * scale
        causal = jnp.tril(jnp.ones((Tlen, Tlen), dtype=bool))
        att = jnp.where(causal[None, None], att, -jnp.inf)
        att = jax.nn.softmax(att, axis=-1)
        y = jnp.einsum('bhts,bsd->bthd', att, v).reshape(Bsz, Tlen, C)
        return y @ Wc_proj

    def _L0_ffn_ref(x, Wg, bg, We, be):
        import jax, jax.numpy as jnp
        import numpy as np
        IN_DIM = 128
        OUT_DIM = 128
        NUM_EXPERTS = 8
        TOP_K = 2
        gate = jax.nn.softmax(x @ Wg + bg, axis=-1)
        topk_vals, topk_idx = jax.lax.top_k(gate, TOP_K)
        onehot = jax.nn.one_hot(topk_idx, NUM_EXPERTS, dtype=gate.dtype)
        gate_sparse = jnp.einsum('bsk,bske->bse', topk_vals, onehot)
        gate_sparse = gate_sparse / jnp.sum(gate_sparse, axis=-1, keepdims=True)
        y = jnp.einsum('bsi,eoi->bseo', x, We) + be[None, None, :, :].transpose(0, 1, 2, 3)
        out = jnp.einsum('bseo,bse->bso', y, gate_sparse)
        return out

    def _L1_attn_ref(x, Wq, bq, Wk, bk, Wv, bv, Wo, bo):
        import jax, jax.numpy as jnp
        import numpy as np
        HIDDEN = 128
        HEADS = 16
        HEAD_DIM = HIDDEN // HEADS
        ROPE_BASE = 10000.0

        def _rope_cos_sin(seq_len, dim):
            inv_freq = 1.0 / ROPE_BASE ** (jnp.arange(0, dim, 2, dtype=jnp.float32) / dim)
            t = jnp.arange(seq_len, dtype=jnp.float32)
            freqs = jnp.einsum('i,j->ij', t, inv_freq)
            emb = jnp.concatenate([freqs, freqs], axis=-1)
            return (jnp.cos(emb), jnp.sin(emb))

        def _apply_rope(x, cos, sin):
            x1, x2 = (x[..., 0::2], x[..., 1::2])
            c = cos[..., :x1.shape[-1]]
            s = sin[..., :x1.shape[-1]]
            return jnp.concatenate([x1 * c - x2 * s, x1 * s + x2 * c], axis=-1)
        B, S, _ = x.shape
        scale = HEAD_DIM ** (-0.5)

        def proj(W, b):
            y = jnp.einsum('bsd,ed->bse', x, W) + b
            return y.reshape(B, S, HEADS, HEAD_DIM).transpose(0, 2, 1, 3)
        q = proj(Wq, bq)
        k = proj(Wk, bk)
        v = proj(Wv, bv)
        cos, sin = _rope_cos_sin(S, HEAD_DIM)
        cos = cos[None, None]
        sin = sin[None, None]
        q = _apply_rope(q, cos, sin) * scale
        k = _apply_rope(k, cos, sin)
        attn = jnp.einsum('bhsd,bhtd->bhst', q, k)
        attn = jax.nn.softmax(attn, axis=-1)
        out = jnp.einsum('bhst,bhtd->bhsd', attn, v)
        out = out.transpose(0, 2, 1, 3).reshape(B, S, HIDDEN)
        return jnp.einsum('bsd,ed->bse', out, Wo) + bo

    def _L1_ffn_ref(x, W_r, W_k, W_v, mu_r, mu_k):
        import jax, jax.numpy as jnp
        import numpy as np
        DIM = 128

        def _reference_tuple_inner(x, W_r, W_k, W_v, mu_r, mu_k):
            B, T, C = x.shape
            x_prev = jnp.concatenate([jnp.zeros((B, 1, C), x.dtype), x[:, :-1, :]], axis=1)
            xr = mu_r * x + (1.0 - mu_r) * x_prev
            xk = mu_k * x + (1.0 - mu_k) * x_prev
            r = jax.nn.sigmoid(jnp.einsum('btc,dc->btd', xr, W_r))
            k = jnp.einsum('btc,dc->btd', xk, W_k)
            k_act = jnp.square(jax.nn.relu(k))
            out = r * jnp.einsum('btc,dc->btd', k_act, W_v)
            new_state = x[:, -1, :]
            return (out, new_state)
        return _reference_tuple_inner(x, W_r, W_k, W_v, mu_r, mu_k)[0]

    def _L2_attn_ref(hidden_states, Wq, bq, Wk, bk, Wv, bv, Wf, bf, Wo, bo):
        import jax, jax.numpy as jnp
        import numpy as np
        S_LEN, BATCH, HID, HEADS = (256, 4, 128, 16)
        HD = HID // HEADS

        def _forget_attention(hidden_states, Wq, bq, Wk, bk, Wv, bv, Wf, bf, Wo, bo):
            S, B, H = hidden_states.shape
            nh, hd = (HEADS, HD)

            def shape(x):
                return x.reshape(S, B, nh, hd)
            q = shape(hidden_states @ Wq.T + bq)
            k = shape(hidden_states @ Wk.T + bk)
            v = shape(hidden_states @ Wv.T + bv)
            phi_q = jax.nn.elu(q) + 1.0
            phi_k = jax.nn.elu(k) + 1.0
            f = jax.nn.sigmoid(hidden_states @ Wf.T + bf)

            def step(carry, xs):
                Sm, z = carry
                ft, pk, pq, vt = xs
                fte = ft[..., None]
                Sm = fte[..., None] * Sm + pk[..., :, None] * vt[..., None, :]
                z = fte * z + pk
                num = jnp.einsum('bhd,bhde->bhe', pq, Sm)
                den = jnp.einsum('bhd,bhd->bh', pq, z)[..., None]
                return ((Sm, z), num / (den + 1e-06))
            init = (jnp.zeros((B, nh, hd, hd), hidden_states.dtype), jnp.zeros((B, nh, hd), hidden_states.dtype))
            _, out = jax.lax.scan(step, init, (f, phi_k, phi_q, v))
            out = out.reshape(S, B, H) @ Wo.T + bo
            return (out, f)

        def _reference_tuple_inner(hidden_states, Wq, bq, Wk, bk, Wv, bv, Wf, bf, Wo, bo):
            out, f = _forget_attention(hidden_states, Wq, bq, Wk, bk, Wv, bv, Wf, bf, Wo, bo)
            return (out, jnp.zeros_like(out), f)
        return _reference_tuple_inner(hidden_states, Wq, bq, Wk, bk, Wv, bv, Wf, bf, Wo, bo)[0]

    def _L2_ffn_ref(x, w_gate, w_up, w_down):
        import jax, jax.numpy as jnp
        import numpy as np
        DIM = 128
        HIDDEN = 384
        SCALE = 1.0 / 127.0

        def _dequant(w_int, dtype):
            return w_int.astype(dtype) * jnp.asarray(SCALE, dtype)
        wg = _dequant(w_gate, x.dtype)
        wu = _dequant(w_up, x.dtype)
        wd = _dequant(w_down, x.dtype)
        gate = jnp.einsum('bsd,hd->bsh', x, wg)
        up = jnp.einsum('bsd,hd->bsh', x, wu)
        h = jax.nn.silu(gate) * up
        return jnp.einsum('bsh,dh->bsd', h, wd)

    def _L3_attn_ref(x, time_decay, time_first, time_mix_k, time_mix_v, time_mix_r, Wk, Wv, Wr, Wo):
        import jax, jax.numpy as jnp
        import numpy as np
        import math
        B, T, C, D = (8, 256, 128, 128)
        N_LAYER, LAYER_ID = (24, 12)

        def _wkv(time_decay, time_first, k, v):
            ew = jnp.exp(-jnp.exp(time_decay))
            eu = jnp.exp(time_first)
            ek = jnp.exp(k)
            ekv = ek * v

            def step(carry, inp):
                a, b = carry
                ekt, ekvt = inp
                out = (eu * ekvt + a) / (eu * ekt + b)
                return ((ew * a + ekvt, ew * b + ekt), out)
            init = (jnp.zeros_like(ek[:, 0]), jnp.zeros_like(ek[:, 0]))
            xs = (jnp.swapaxes(ek, 0, 1), jnp.swapaxes(ekv, 0, 1))
            _, out = jax.lax.scan(step, init, xs)
            return jnp.swapaxes(out, 0, 1)
        xx = jnp.pad(x, ((0, 0), (1, 0), (0, 0)))[:, :-1]
        xk = x * time_mix_k + xx * (1 - time_mix_k)
        xv = x * time_mix_v + xx * (1 - time_mix_v)
        xr = x * time_mix_r + xx * (1 - time_mix_r)
        k = jnp.einsum('btc,dc->btd', xk, Wk)
        v = jnp.einsum('btc,dc->btd', xv, Wv)
        sr = jax.nn.sigmoid(jnp.einsum('btc,dc->btd', xr, Wr))
        rwkv = sr * _wkv(time_decay, time_first, k, v)
        return jnp.einsum('btd,cd->btc', rwkv, Wo)

    def _L3_ffn_ref(x, Wqkv, q_scale, k_scale, Wo, ln_g, ln_b, W1, b1, W2, b2):
        import jax, jax.numpy as jnp
        import numpy as np
        DIM = 128
        DEPTH = 6
        HEADS = 16
        DIM_HEAD = 64
        WINDOW = 32
        INNER = HEADS * DIM_HEAD
        DIM_INNER = int(DIM * 4 * 2 / 3)
        QK_SCALE = 8.0

        def shift_tokens(t):
            a, s = jnp.split(t, 2, -1)
            s = jnp.pad(s, ((0, 0), (1, 0), (0, 0)))[:, :-1]
            return jnp.concatenate([a, s], -1)

        def l2norm(t):
            return t / jnp.maximum(jnp.linalg.norm(t, axis=-1, keepdims=True), 1e-12)

        def rotate_half(x):
            x1, x2 = jnp.split(x, 2, -1)
            return jnp.concatenate([-x2, x1], -1)

        def rotary_tables(n):
            half = jnp.arange(0, DIM_HEAD, 2, dtype=jnp.float32)
            inv_freq = 1.0 / 10000.0 ** (half / DIM_HEAD)
            t = jnp.arange(n, dtype=jnp.float32)
            freqs = t[:, None] * inv_freq[None, :]
            freqs = jnp.concatenate([freqs, freqs], -1)
            base_scale = (half + 0.4 * DIM_HEAD) / (1.4 * DIM_HEAD)
            power = (t - n // 2) / (WINDOW // 2)
            scale = base_scale[None, :] ** power[:, None]
            scale = jnp.concatenate([scale, scale], -1)
            return (freqs, scale)

        def local_attention(q, k, v):
            b, h, n, d = q.shape
            w = WINDOW
            nw = n // w
            bq = q.reshape(b, h, nw, w, d)
            bk = k.reshape(b, h, nw, w, d)
            bv = v.reshape(b, h, nw, w, d)

            def look(t):
                p = jnp.pad(t, ((0, 0), (0, 0), (1, 0), (0, 0), (0, 0)))
                return jnp.concatenate([p[:, :, :nw], p[:, :, 1:]], axis=3)
            bk2, bv2 = (look(bk), look(bv))
            seq = jnp.arange(n).reshape(nw, w)
            seq_p = jnp.pad(seq, ((1, 0), (0, 0)), constant_values=-1)
            jt = jnp.concatenate([seq_p[:nw], seq_p[1:]], axis=1)
            it = seq[:, :, None]
            jb = jt[:, None, :]
            mask = (it < jb) | (it > jb + w) | (jb == -1)
            sim = jnp.einsum('bhwie,bhwje->bhwij', bq, bk2) * QK_SCALE
            sim = jnp.where(mask, -jnp.finfo(sim.dtype).max, sim)
            attn = jax.nn.softmax(sim, -1)
            out = jnp.einsum('bhwij,bhwje->bhwie', attn, bv2)
            return out.reshape(b, h, n, d)

        def attn_layer(x, Wqkv, qs, ksc, Wo):
            b, n, _ = x.shape
            qkv = x @ Wqkv
            q, k, v = jnp.split(qkv, 3, -1)
            sh = lambda t: t.reshape(b, n, HEADS, DIM_HEAD).transpose(0, 2, 1, 3)
            q, k, v = (sh(q), sh(k), sh(v))
            q = l2norm(q) * qs
            k = l2norm(k) * ksc
            freqs, scale = rotary_tables(n)
            cos, sin = (jnp.cos(freqs), jnp.sin(freqs))
            q = q * cos * scale + rotate_half(q) * sin * scale
            inv = 1.0 / scale
            k = k * cos * inv + rotate_half(k) * sin * inv
            out = local_attention(q, k, v)
            out = out.transpose(0, 2, 1, 3).reshape(b, n, INNER)
            return out @ Wo

        def ffn_layer(x, g, bln, W1, b1, W2, b2):
            mu = x.mean(-1, keepdims=True)
            var = ((x - mu) ** 2).mean(-1, keepdims=True)
            xn = (x - mu) / jnp.sqrt(var + 1e-05) * g + bln
            hg = xn @ W1 + b1
            a, gate = jnp.split(hg, 2, -1)
            return a * jax.nn.gelu(gate, approximate=False) @ W2 + b2
        for i in range(DEPTH):
            x = attn_layer(shift_tokens(x), Wqkv[i], q_scale[i], k_scale[i], Wo[i]) + x
            x = ffn_layer(shift_tokens(x), ln_g[i], ln_b[i], W1[i], b1[i], W2[i], b2[i]) + x
        return x
    x = L0_attn_x
    x = x + 0.5 * _L0_ffn_ref(_layernorm(x, axis=-1), L0_ffn_Wg, L0_ffn_bg, L0_ffn_We, L0_ffn_be)
    x = x + _L0_attn_ref(_layernorm(x, axis=-1), L0_attn_Wc_down, L0_attn_Wq_up, L0_attn_Wkv_up, L0_attn_Wc_proj)
    x = x + 0.5 * _L0_ffn_ref(_layernorm(x, axis=-1), L0_ffn_Wg, L0_ffn_bg, L0_ffn_We, L0_ffn_be)
    x = x + 0.5 * _L1_ffn_ref(_layernorm(x, axis=-1), L1_ffn_W_r, L1_ffn_W_k, L1_ffn_W_v, L1_ffn_mu_r, L1_ffn_mu_k)
    x = x + _L1_attn_ref(_layernorm(x, axis=-1), L1_attn_Wq, L1_attn_bq, L1_attn_Wk, L1_attn_bk, L1_attn_Wv, L1_attn_bv, L1_attn_Wo, L1_attn_bo)
    x = x + 0.5 * _L1_ffn_ref(_layernorm(x, axis=-1), L1_ffn_W_r, L1_ffn_W_k, L1_ffn_W_v, L1_ffn_mu_r, L1_ffn_mu_k)
    x = x + 0.5 * _L2_ffn_ref(_layernorm(x, axis=-1), L2_ffn_w_gate, L2_ffn_w_up, L2_ffn_w_down)
    x = x + _L2_attn_ref(_layernorm(x, axis=-1), L2_attn_Wq, L2_attn_bq, L2_attn_Wk, L2_attn_bk, L2_attn_Wv, L2_attn_bv, L2_attn_Wf, L2_attn_bf, L2_attn_Wo, L2_attn_bo)
    x = x + 0.5 * _L2_ffn_ref(_layernorm(x, axis=-1), L2_ffn_w_gate, L2_ffn_w_up, L2_ffn_w_down)
    x = x + 0.5 * _L3_ffn_ref(_layernorm(x, axis=-1), L3_ffn_Wqkv, L3_ffn_q_scale, L3_ffn_k_scale, L3_ffn_Wo, L3_ffn_ln_g, L3_ffn_ln_b, L3_ffn_W1, L3_ffn_b1, L3_ffn_W2, L3_ffn_b2)
    x = x + _L3_attn_ref(_layernorm(x, axis=-1), L3_attn_time_decay, L3_attn_time_first, L3_attn_time_mix_k, L3_attn_time_mix_v, L3_attn_time_mix_r, L3_attn_Wk, L3_attn_Wv, L3_attn_Wr, L3_attn_Wo)
    x = x + 0.5 * _L3_ffn_ref(_layernorm(x, axis=-1), L3_ffn_Wqkv, L3_ffn_q_scale, L3_ffn_k_scale, L3_ffn_Wo, L3_ffn_ln_g, L3_ffn_ln_b, L3_ffn_W1, L3_ffn_b1, L3_ffn_W2, L3_ffn_b2)
    return x

_drawn_inputs = setup_inputs


def setup_inputs(seed=0):
    import zlib

    import numpy as np

    out = dict(_drawn_inputs(seed))
    spreads = {'L0_ffn_bg': (0.0, 0.1),
     'L2_attn_bq': (0.0, 0.1),
     'L2_attn_bk': (0.0, 0.1),
     'L2_attn_bv': (0.0, 0.1),
     'L2_attn_bf': (0.0, 0.1),
     'L2_attn_bo': (0.0, 0.1),
     'L3_ffn_q_scale': (1.0, 0.2),
     'L3_ffn_k_scale': (1.0, 0.2),
     'L3_ffn_ln_g': (1.0, 0.2),
     'L3_ffn_ln_b': (0.0, 0.1),
     'L3_ffn_b1': (0.0, 0.1),
     'L3_ffn_b2': (0.0, 0.1)}
    factors = {}
    for name, (base, spread) in spreads.items():
        noise = np.random.default_rng([zlib.crc32(name.encode()), seed]).standard_normal(out[name].shape)
        drawn = base * np.exp(spread * noise) if base else spread * noise
        out[name] = jnp.asarray(drawn.astype(out[name].dtype))
    for name, factor in factors.items():
        out[name] = (out[name] * factor).astype(out[name].dtype)
    return out
```

```python
from collections import namedtuple
from contextlib import ExitStack

import concourse.bass as bass
from concourse import mybir

F32 = mybir.dt.float32
BF16 = mybir.dt.bfloat16
I32 = mybir.dt.int32
ALU = mybir.AluOpType
ACT = mybir.ActivationFunctionType
AX = mybir.AxisListType

P = 128
NB, T = 4, 512
TILES = T // P
HEADS8, HD8 = 16, 8
QUADS, PERQ = 4, 4
EXPERTS = 8
HID = 384
HBLK = HID // P
DEPTH, LHEADS, LD, WIN = 6, 16, 64, 32
PAIRS = LHEADS // 2
INNER = LHEADS * LD
WPT = P // WIN
DI = 341
DIB = [(0, 128), (128, 128), (256, DI - 256)]
LN_EPS = 1e-5
NORM_FLOOR = 1e-24
FAR = 1e30


ARENA = 20000

SUBLAYERS = ["moe", "mqa", "moe", "chan", "rope", "chan", "swiglu", "forget", "swiglu", "deep", "time", "deep"]


def program(nc, d, out, sublayers):
    with ExitStack() as ctx:
        def sb(name, shape, dt=F32):
            return ctx.enter_context(nc.sbuf_tensor(name, shape, dt))

        psum = ctx.enter_context(nc.psum_tensor("psum", [P, 8 * 512], F32))

        def bank(i):
            return psum[:, i * 512:(i + 1) * 512]

        def banks(i, n):
            return psum[:, i * 512:(i + n) * 512].rearrange("p (n c) -> p n c", c=512)

        fixed = [n for n in d if n != "x" and not n.startswith("deep_")]
        passing = ["later_key_q", "later_key_k", "sw_gate", "sw_up", "sw_down"]
        kept = {n: sb("w_" + n, list(d[n].shape), d[n].dtype) for n in fixed if n not in passing}
        w = namedtuple("Weights", kept)(**kept)
        identb = sb("identb", [P, P], BF16)
        later_key_q = sb("later_key_q", [P, P], BF16)
        later_key_k = sb("later_key_k", [P, P], BF16)
        layered = [n for n in d if n.startswith("deep_")]
        deep_kept = [{n: sb(f"{n}_{h}", list(d[n].shape[1:])) for n in layered} for h in range(2)]
        deep_w = [namedtuple("Layer", [n[5:] for n in layered])(*deep_kept[h].values()) for h in range(2)]

        x = sb("x", [P, NB * T])
        z = sb("z", [P, NB * T])
        eps = sb("eps", [P, 1])
        xc = sb("xc", [P, T])
        xc_sq = sb("xc_sq", [P, T])
        std = sb("std", [P, TILES])
        rstd = sb("rstd", [P, TILES])
        xn = sb("xn", [P, 1 + T])
        xn_now, xn_prev = xn[:, 1:1 + T], xn[:, 0:T]
        xs = sb("xs", [P, WIN + T])
        xs_now = xs[:, WIN:WIN + T]
        mx = sb("mx", [P, TILES, P])
        state = sb("state", [P, 2, 1 + T])
        deep_kT = sb("deep_kT", [P, PAIRS, WIN + T])
        ew = sb("ew", [P, 1])
        eu = sb("eu", [P, 1])
        gate_w = sb("gate_w", [P, HID])
        up_w = sb("up_w", [P, HID])
        down_w = sb("down_w", [P, HBLK, P])

        arena = sb("arena", [P, ARENA])
        top = [0]

        def new(*shape):
            size = 1
            for s in shape:
                size *= s
            a = arena[:, top[0]:top[0] + size]
            top[0] += size
            assert top[0] <= ARENA, top[0]
            if len(shape) == 2:
                a = a.rearrange("p (a b) -> p a b", b=shape[1])
            elif len(shape) == 3:
                a = a.rearrange("p (a b c) -> p a b c", b=shape[1], c=shape[2])
            return a

        raw = {n: new(*d[n].shape[1:]).bitcast(d[n].dtype) for n in passing}

        def apart(eng):
            eng.sem_inc(g.waits_passed, 1)

        def sems(names):
            names = names.split()
            return namedtuple("Semaphores", names)(*[ctx.enter_context(nc.semaphore(n)) for n in names])

        def link(eng, counter, base):
            n = [0]

            def step(ins):
                n[0] += 1
                ins.then_inc(counter, 1)
                eng.wait_ge(counter, base + n[0])
            return step, n

        g = sems("waits_passed weights_loaded x_loaded pads_zeroed weights_scaled unit_done stored")
        ln = sems("ln_mean_ready ln_centred ln_squared ln_var_ready ln_std_ready ln_rstd_ready ln_rstd_spread ln_normed")

        def unit(b):
            return bass.ds(b * T, T)

        def ln_pe(pe, n, src):
            nc.tensor.matmul(bank(4), w.avg[:, :], src, start=True, stop=True).then_inc(ln.ln_mean_ready, 1)
            pe.wait_ge(ln.ln_squared, n + 1)
            for t in range(TILES):
                last = nc.tensor.matmul(bank(5)[:, t:t + 1], xc_sq[:, t * P:(t + 1) * P], w.avg[:, 0:1],
                                        start=True, stop=True)
            last.then_inc(ln.ln_var_ready, 1)
            pe.wait_ge(ln.ln_rstd_ready, n + 1)
            for t in range(TILES):
                last = nc.tensor.matmul(bank(4)[:, t * P:(t + 1) * P], rstd[:, t:t + 1].broadcast_to([P, P]),
                                        w.ident[:, :], start=True, stop=True)
            last.then_inc(ln.ln_rstd_spread, 1)

        def ln_act(act, n):
            act.wait_ge(ln.ln_centred, n + 1)
            nc.scalar.activation(xc_sq[:, :], xc[:, :], ACT.Square).then_inc(ln.ln_squared, 1)
            act.wait_ge(ln.ln_var_ready, n + 1)
            nc.scalar.activation(std[:, :], bank(5)[:, 0:TILES], ACT.Sqrt, bias=eps[:, :]).then_inc(ln.ln_std_ready, 1)

        def ln_dve(dve, n, src, dst):
            dve.wait_ge(ln.ln_mean_ready, n + 1)
            nc.vector.tensor_tensor(xc[:, :], src, bank(4), ALU.subtract).then_inc(ln.ln_centred, 1)
            dve.wait_ge(ln.ln_std_ready, n + 1)
            nc.vector.reciprocal(rstd[:, :], std[:, :]).then_inc(ln.ln_rstd_ready, 1)
            dve.wait_ge(ln.ln_rstd_spread, n + 1)
            dve.wait_ge(ln.ln_centred, n + 1)
            nc.vector.tensor_tensor(dst, xc[:, :], bank(4), ALU.mult).then_inc(ln.ln_normed, 1)

        cm = sems("cm_step cm_mixed cm_r_ready cm_k_ready cm_r_done cm_relu_done cm_squared cm_v_ready")
        top[0] = 0
        cm_d, cm_r, cm_k, cm_gate, cm_relu, cm_sq, cm_out = (new(T) for _ in range(7))
        CM_STEPS = 2

        def chan_pe(pe, u, n, k, b):
            pe.wait_ge(g.unit_done, u)
            ln_pe(pe, n, x[:, unit(b)])
            pe.wait_ge(cm.cm_mixed, 2 * k + 2)
            nc.tensor.matmul(bank(0), w.cm_wr[:, :], cm_r, start=True, stop=True).then_inc(cm.cm_r_ready, 1)
            nc.tensor.matmul(bank(1), w.cm_wk[:, :], cm_k, start=True, stop=True).then_inc(cm.cm_k_ready, 1)
            pe.wait_ge(cm.cm_squared, k + 1)
            nc.tensor.matmul(bank(2), w.cm_wv[:, :], cm_sq, start=True, stop=True).then_inc(cm.cm_v_ready, 1)

        def chan_act(act, u, n, k, b):
            ln_act(act, n)
            act.wait_ge(cm.cm_r_ready, k + 1)
            nc.scalar.activation(cm_gate, bank(0), ACT.Sigmoid).then_inc(cm.cm_r_done, 1)
            act.wait_ge(cm.cm_k_ready, k + 1)
            nc.scalar.activation(cm_relu, bank(1), ACT.Relu).then_inc(cm.cm_relu_done, 1)

        def chan_dve(dve, u, n, k, b):
            ln_dve(dve, n, x[:, unit(b)], xn_now)
            step, steps = link(dve, cm.cm_step, CM_STEPS * k)
            dve.wait_ge(ln.ln_normed, n + 1)
            step(nc.vector.tensor_tensor(cm_d, xn_now, xn_prev, ALU.subtract))
            for mu, dst in ((w.cm_mu_r, cm_r), (w.cm_mu_k, cm_k)):
                nc.vector.scalar_tensor_tensor(dst, cm_d, mu[:, 0:1], xn_prev, ALU.mult, ALU.add).then_inc(cm.cm_mixed, 1)
            dve.wait_ge(cm.cm_relu_done, k + 1)
            nc.vector.tensor_tensor(cm_sq, cm_relu, cm_relu, ALU.mult).then_inc(cm.cm_squared, 1)
            dve.wait_ge(cm.cm_r_done, k + 1)
            dve.wait_ge(cm.cm_v_ready, k + 1)
            step(nc.vector.tensor_tensor(cm_out, bank(2), cm_gate, ALU.mult))
            nc.vector.scalar_tensor_tensor(x[:, unit(b)], cm_out, 0.5, x[:, unit(b)], ALU.mult, ALU.add).then_inc(g.unit_done, 1)
            dve.wait_ge(g.unit_done, u + 1)
            assert steps[0] == CM_STEPS

        sw = sems("sw_gate_ready sw_up_ready sw_silu_done sw_gated sw_down_ready")
        top[0] = 0
        sw_silu, sw_h = new(HBLK, T), new(HBLK, T)
        SW_UP = [3, 5, 6]

        def swiglu_pe(pe, u, n, k, b):
            pe.wait_ge(g.unit_done, u)
            ln_pe(pe, n, x[:, unit(b)])
            pe.wait_ge(ln.ln_normed, n + 1)
            for j in range(HBLK):
                nc.tensor.matmul(bank(j), gate_w[:, j * P:(j + 1) * P], xn_now, start=True, stop=True).then_inc(sw.sw_gate_ready, 1)
                nc.tensor.matmul(bank(SW_UP[j]), up_w[:, j * P:(j + 1) * P], xn_now, start=True, stop=True).then_inc(sw.sw_up_ready, 1)
            for j in range(HBLK):
                pe.wait_ge(sw.sw_gated, HBLK * k + j + 1)
                last = nc.tensor.matmul(bank(7), down_w[:, j, :], sw_h[:, j, :], start=(j == 0), stop=(j == HBLK - 1))
            last.then_inc(sw.sw_down_ready, 1)

        def swiglu_act(act, u, n, k, b):
            ln_act(act, n)
            for j in range(HBLK):
                act.wait_ge(sw.sw_gate_ready, HBLK * k + j + 1)
                nc.scalar.activation(sw_silu[:, j, :], bank(j), ACT.Silu).then_inc(sw.sw_silu_done, 1)

        def swiglu_dve(dve, u, n, k, b):
            ln_dve(dve, n, x[:, unit(b)], xn_now)
            for j in range(HBLK):
                dve.wait_ge(sw.sw_silu_done, HBLK * k + j + 1)
                dve.wait_ge(sw.sw_up_ready, HBLK * k + j + 1)
                nc.vector.tensor_tensor(sw_h[:, j, :], bank(SW_UP[j]), sw_silu[:, j, :], ALU.mult).then_inc(sw.sw_gated, 1)
            dve.wait_ge(sw.sw_down_ready, k + 1)
            nc.vector.scalar_tensor_tensor(x[:, unit(b)], bank(7), 0.5, x[:, unit(b)], ALU.mult, ALU.add).then_inc(g.unit_done, 1)
            dve.wait_ge(g.unit_done, u + 1)

        mo = sems("moe_logits_ready moe_step moe_shifted moe_exped moe_gates_ready moe_gates_turned moe_gates_kept "
                  "moe_experts_ready moe_weighted moe_summed moe_out_ready")
        top[0] = 0
        G = [P, TILES, EXPERTS]
        lo, eq, rank, one1, lo2, one2, ex, gates = (new(TILES, EXPERTS) for _ in range(8))
        m1, m2, r1, r2, gsum, ginv = (new(TILES) for _ in range(6))
        gatesT = new(T)
        moe_prod, moe_acc = new(EXPERTS, P), new(2, P)
        MOE_STEPS = 14

        def over(a, shape):
            return a.rearrange("p (n o) -> p n o", o=1).broadcast_to(shape)

        def under(a, shape):
            return a.rearrange("p (o c) -> p o c", o=1).broadcast_to(shape)

        def moe_pe(pe, u, n, k, b):
            pe.wait_ge(g.unit_done, u)
            ln_pe(pe, n, x[:, unit(b)])
            pe.wait_ge(ln.ln_normed, n + 1)
            for t in range(TILES):
                last = nc.tensor.matmul(bank(5)[:, t * EXPERTS:(t + 1) * EXPERTS], xn[:, 1 + t * P:1 + (t + 1) * P],
                                        w.moe_wg[:, :], start=True, stop=True)
            last.then_inc(mo.moe_logits_ready, 1)
            for t in range(TILES):
                a = 2 * (t % 2)
                if t >= 2:
                    pe.wait_ge(mo.moe_weighted, TILES * k + t - 1)
                for h in range(2):
                    last = nc.tensor.matmul(bank(a + h), xn[:, 1 + t * P:1 + (t + 1) * P],
                                            w.moe_we[:, 4 * h:4 * h + 4, :], start=True, stop=True)
                last.then_inc(mo.moe_experts_ready, 1)
                if t == 0:
                    pe.wait_ge(mo.moe_gates_ready, k + 1)
                    for tt in range(TILES):
                        last = nc.tensor.matmul(bank(6)[0:EXPERTS, tt * P:(tt + 1) * P], gates[:, tt, :], w.ident[:, :],
                                                start=True, stop=True)
                    last.then_inc(mo.moe_gates_turned, 1)
                    pe.wait_ge(mo.moe_gates_kept, k + 1)
                    nc.tensor.matmul(bank(7), w.moe_be[:, :], gatesT[0:EXPERTS, :], start=True, stop=False, skip_group_check=True)
                if t >= 1:
                    moe_turn(pe, k, t - 1)
            moe_turn(pe, k, TILES - 1)

        def moe_turn(pe, k, t):
            pe.wait_ge(mo.moe_summed, TILES * k + t + 1)
            last = nc.tensor.matmul(bank(7)[:, t * P:(t + 1) * P], moe_acc[:, t % 2, :], w.ident[:, :],
                                    start=False, stop=(t == TILES - 1), skip_group_check=True)
            last.then_inc(mo.moe_out_ready, 1)

        def moe_act(act, u, n, k, b):
            ln_act(act, n)
            act.wait_ge(mo.moe_shifted, k + 1)
            nc.scalar.activation(ex, lo2, ACT.Exp).then_inc(mo.moe_exped, 1)
            act.wait_ge(mo.moe_gates_turned, k + 1)
            nc.scalar.activation(gatesT[0:EXPERTS, :], bank(6)[0:EXPERTS, :], ACT.Copy).then_inc(mo.moe_gates_kept, 1)

        def moe_dve(dve, u, n, k, b):
            ln_dve(dve, n, x[:, unit(b)], xn_now)
            step, steps = link(dve, mo.moe_step, MOE_STEPS * k)
            dve.wait_ge(mo.moe_logits_ready, k + 1)
            step(nc.vector.tensor_tensor(lo, bank(5)[:, 0:TILES * EXPERTS].rearrange("p (t e) -> p t e", e=EXPERTS),
                                         under(w.moe_bg[:, :], G), ALU.add))
            step(nc.vector.tensor_reduce(m1, lo, AX.X, ALU.max))
            step(nc.vector.tensor_tensor(eq, lo, over(m1, G), ALU.is_equal))
            step(nc.vector.tensor_tensor(rank, eq, under(w.moe_order[:, :], G), ALU.mult))
            step(nc.vector.tensor_reduce(r1, rank, AX.X, ALU.max))
            step(nc.vector.tensor_tensor(one1, rank, over(r1, G), ALU.is_equal))
            step(nc.vector.scalar_tensor_tensor(lo2, one1, -FAR, lo, ALU.mult, ALU.add))
            step(nc.vector.tensor_reduce(m2, lo2, AX.X, ALU.max))
            step(nc.vector.tensor_tensor(eq, lo2, over(m2, G), ALU.is_equal))
            step(nc.vector.tensor_tensor(rank, eq, under(w.moe_order[:, :], G), ALU.mult))
            step(nc.vector.tensor_reduce(r2, rank, AX.X, ALU.max))
            nc.vector.tensor_tensor(lo2, lo, over(m1, G), ALU.subtract).then_inc(mo.moe_shifted, 1)
            step(nc.vector.tensor_tensor(one2, rank, over(r2, G), ALU.is_equal))
            step(nc.vector.tensor_tensor(one1, one1, one2, ALU.add))
            dve.wait_ge(mo.moe_exped, k + 1)
            nc.vector.tensor_tensor(ex, ex, one1, ALU.mult).then_inc(mo.moe_step, 1)
            dve.wait_ge(mo.moe_step, MOE_STEPS * k + MOE_STEPS)
            steps[0] += 1
            assert steps[0] == MOE_STEPS
            nc.vector.tensor_reduce(gsum, ex, AX.X, ALU.add).then_inc(mo2.moe_gsum, 1)
            dve.wait_ge(mo2.moe_gsum, k + 1)
            nc.vector.reciprocal(ginv, gsum).then_inc(mo2.moe_ginv, 1)
            dve.wait_ge(mo2.moe_ginv, k + 1)
            nc.vector.tensor_tensor(gates, ex, over(ginv, G), ALU.mult).then_inc(mo.moe_gates_ready, 1)
            dve.wait_ge(mo.moe_gates_ready, k + 1)
            for t in range(TILES):
                a = 2 * (t % 2)
                dve.wait_ge(mo.moe_experts_ready, TILES * k + t + 1)
                nc.vector.tensor_tensor(moe_prod, psum[:, a * 512:(a + 2) * 512].rearrange("p (e o) -> p e o", o=P),
                                        over(gates[:, t, :], [P, EXPERTS, P]), ALU.mult).then_inc(mo.moe_weighted, 1)
                dve.wait_ge(mo.moe_weighted, TILES * k + t + 1)
                if t >= 2:
                    dve.wait_ge(mo.moe_out_ready, TILES * k + t - 1)
                nc.vector.tensor_reduce(moe_acc[:, t % 2, :], moe_prod.rearrange("p e o -> p o e"), AX.X,
                                        ALU.add).then_inc(mo.moe_summed, 1)
                dve.wait_ge(mo.moe_summed, TILES * k + t + 1)
            dve.wait_ge(mo.moe_out_ready, TILES * k + TILES)
            nc.vector.scalar_tensor_tensor(x[:, unit(b)], bank(7), 0.5, x[:, unit(b)], ALU.mult, ALU.add).then_inc(g.unit_done, 1)
            dve.wait_ge(g.unit_done, u + 1)

        mo2 = sems("moe_gsum moe_ginv")

        da = sems("da_latent_ready da_latent_kept da_q_ready da_k_ready da_v_ready da_qb_kept da_kb_kept da_rot_ready "
                  "da_roped da_step da_q_kept da_kt_kept da_v_kept da_vm_kept da_scores_ready da_max_kept "
                  "da_max_turned da_max_copied da_st_ready da_probs_ready da_pv_done da_inv_kept da_y_ready da_out_ready")
        top[0] = 0
        da_lat, da_qT, da_kT, da_rotq, da_t1, da_t2 = new(T), new(T), new(T), new(T), new(T), new(T)
        da_kb = new(T)
        da_kTm = new(PERQ, T)
        da_V = new(TILES, P)
        da_Vm = new(PERQ, TILES, P)
        da_nm = new(T)
        da_PT = new(2, QUADS, T)
        da_inv, da_y = new(T), new(T)

        def dense_pe(pe, u, n, k, b, causal, other):
            A = TILES * PERQ
            pe.wait_ge(g.unit_done, u)
            ln_pe(pe, n, x[:, unit(b)])
            pe.wait_ge(ln.ln_normed, n + 1)
            if causal:
                nc.tensor.matmul(bank(0)[0:64, :], w.mqa_down[:, :], xn_now, start=True, stop=True).then_inc(da.da_latent_ready, 1)
                pe.wait_ge(da.da_latent_kept, (k - other) + 1)
                src, wq, wk, wv = da_lat[0:64, :], w.mqa_q, w.mqa_k, w.mqa_v
            else:
                src, wq, wk, wv = xn_now, w.ra_wq, w.ra_wk, w.ra_wv
            nc.tensor.matmul(bank(1), wq[:, :], src, start=True, stop=True).then_inc(da.da_q_ready, 1)
            nc.tensor.matmul(bank(2), wk[:, :], src, start=True, stop=True).then_inc(da.da_k_ready, 1)
            for t in range(TILES):
                last = nc.tensor.matmul(bank(3)[:, t * P:(t + 1) * P], src[:, t * P:(t + 1) * P], wv[:, :], start=True, stop=True)
            last.then_inc(da.da_v_ready, 1)
            if not causal:
                pe.wait_ge(da.da_qb_kept, (k - other) + 1)
                nc.tensor.matmul(bank(6), w.rot8[:, :], da_qT, start=True, stop=True).then_inc(da.da_rot_ready, 1)
                pe.wait_ge(da.da_kb_kept, (k - other) + 1)
                nc.tensor.matmul(bank(7), w.rot8[:, :], da_kb, start=True, stop=True).then_inc(da.da_rot_ready, 1)
            pe.wait_ge(da.da_q_kept, k + 1)
            pe.wait_ge(da.da_kt_kept, PERQ * k + PERQ)
            pe.wait_ge(da.da_vm_kept, PERQ * k + PERQ)
            for qt in range(TILES):
                keys = (qt + 1) * P if causal else T
                for gg in range(PERQ):
                    i = PERQ * qt + gg
                    a = 4 * (i % 2)
                    if i >= 2:
                        pe.wait_ge(da.da_max_kept, A * k + i - 1)
                    for j in range(QUADS):
                        q4 = slice(32 * j, 32 * j + 32)
                        last = nc.tensor.matmul(bank(a + j)[:, 0:keys], da_qT[q4, qt * P:(qt + 1) * P],
                                                da_kTm[q4, gg, 0:keys], start=True, stop=not causal)
                        if causal:
                            last = nc.tensor.matmul(bank(a + j)[:, qt * P:keys], identb[:, :], later_key_q[:, :],
                                                    start=False, stop=True)
                    last.then_inc(da.da_scores_ready, 1)
            pe.wait_ge(da.da_max_kept, A * k + A)
            for qt in range(TILES):
                last = nc.tensor.matmul(bank(0)[:, qt * P:(qt + 1) * P], mx[:, qt, :], w.ident[:, :], start=True, stop=True)
            last.then_inc(da.da_max_turned, 1)
            pe.wait_ge(da.da_max_copied, k + 1)
            for i in range(A + 1):
                if i < A:
                    kt, gg = i // PERQ, i % PERQ
                    q0 = kt * P if causal else 0
                    for j in range(QUADS):
                        if i >= 1:
                            pe.wait_ge(da.da_probs_ready, QUADS * (A * k + i - 1) + j + 1)
                        q4 = slice(32 * j, 32 * j + 32)
                        nc.tensor.matmul(bank(j)[:, q0:T], da_kTm[q4, gg, kt * P:(kt + 1) * P], da_qT[q4, q0:T],
                                         start=True, stop=False)
                        last = nc.tensor.matmul(bank(j)[:, q0:T], w.row_of[q4, gg, :], da_nm[q4, q0:T],
                                                start=False, stop=not causal)
                        if causal:
                            last = nc.tensor.matmul(bank(j)[:, q0:q0 + P], identb[:, :], later_key_k[:, :],
                                                    start=False, stop=True)
                        last.then_inc(da.da_st_ready, 1)
                if i >= 1:
                    m = i - 1
                    kt, gg = m // PERQ, m % PERQ
                    q0 = kt * P if causal else 0
                    pe.wait_ge(da.da_probs_ready, QUADS * (A * k + m + 1))
                    for lhs, to in ((da_Vm[:, gg, kt, :], 6), (w.col_of[:, gg, :], 7)):
                        for j in range(QUADS):
                            q4 = slice(32 * j, 32 * j + 32)
                            last = nc.tensor.matmul(bank(to)[q4, q0:T], lhs[:, q4], da_PT[:, m % 2, j, q0:T],
                                                    start=(m == 0), stop=(m == A - 1), skip_group_check=True)
                    last.then_inc(da.da_pv_done, 1)
            pe.wait_ge(da.da_y_ready, k + 1)
            nc.tensor.matmul(bank(1), (w.mqa_proj if causal else w.ra_wo)[:, :], da_y, start=True,
                             stop=True).then_inc(da.da_out_ready, 1)

        def dense_act(act, u, n, k, b, causal, other):
            A = TILES * PERQ
            ln_act(act, n)
            if causal:
                act.wait_ge(da.da_latent_ready, (k - other) + 1)
                nc.scalar.activation(da_lat[0:64, :], bank(0)[0:64, :], ACT.Copy).then_inc(da.da_latent_kept, 1)
                act.wait_ge(da.da_q_ready, k + 1)
                nc.scalar.activation(da_qT, bank(1), ACT.Copy, scale=HD8 ** -0.5).then_inc(da.da_q_kept, 1)
            else:
                act.wait_ge(da.da_q_ready, k + 1)
                nc.scalar.activation(da_qT, bank(1), ACT.Identity, bias=w.ra_bq[:, :]).then_inc(da.da_qb_kept, 1)
                act.wait_ge(da.da_k_ready, k + 1)
                nc.scalar.activation(da_kb, bank(2), ACT.Identity, bias=w.ra_bk[:, :]).then_inc(da.da_kb_kept, 1)
            act.wait_ge(da.da_max_turned, k + 1)
            nc.scalar.activation(da_nm, bank(0), ACT.Copy).then_inc(da.da_max_copied, 1)
            for i in range(A):
                q0 = (i // PERQ) * P if causal else 0
                if i >= 2:
                    act.wait_ge(da.da_pv_done, A * k + i - 1)
                for j in range(QUADS):
                    act.wait_ge(da.da_st_ready, QUADS * (A * k + i) + j + 1)
                    nc.scalar.activation(da_PT[:, i % 2, j, q0:T], bank(j)[:, q0:T], ACT.Exp).then_inc(da.da_probs_ready, 1)

        def dense_dve(dve, u, n, k, b, causal, other):
            A = TILES * PERQ
            ln_dve(dve, n, x[:, unit(b)], xn_now)
            if causal:
                dve.wait_ge(da.da_k_ready, k + 1)
                for gg in range(PERQ):
                    nc.vector.tensor_scalar(da_kTm[:, gg, :], bank(2), w.row_mask[:, gg:gg + 1], None,
                                            ALU.mult).then_inc(da.da_kt_kept, 1)
                dve.wait_ge(da.da_v_ready, k + 1)
                nc.vector.tensor_copy(da_V, bank(3).rearrange("p (t c) -> p t c", c=P)).then_inc(da.da_v_kept, 1)
            else:
                kk = (k - other)
                cos, sin = w.rope8[:, 0, :], w.rope8[:, 1, :]
                dve.wait_ge(da.da_v_ready, k + 1)
                nc.vector.tensor_tensor(da_V, bank(3).rearrange("p (t c) -> p t c", c=P),
                                        under(w.ra_bv[:, :], [P, TILES, P]), ALU.add).then_inc(da.da_v_kept, 1)
                for m, (kept, src, dst) in enumerate(((da.da_qb_kept, da_qT, da_qT), (da.da_kb_kept, da_kb, da_kT))):
                    dve.wait_ge(kept, kk + 1)
                    nc.vector.tensor_tensor(da_t1, src, cos, ALU.mult).then_inc(da.da_step, 1)
                    dve.wait_ge(da.da_rot_ready, 2 * kk + m + 1)
                    nc.vector.tensor_tensor(da_t2, bank(6 + m), sin, ALU.mult).then_inc(da.da_step, 1)
                    dve.wait_ge(da.da_step, 4 * kk + 2 * m + 2)
                    if m == 0:
                        nc.vector.tensor_tensor(da_t1, da_t1, da_t2, ALU.add).then_inc(da.da_roped, 1)
                        dve.wait_ge(da.da_roped, 2 * kk + 1)
                        nc.vector.tensor_scalar(dst, da_t1, HD8 ** -0.5, None, ALU.mult).then_inc(da.da_q_kept, 1)
                        dve.wait_ge(da.da_q_kept, k + 1)
                    else:
                        nc.vector.tensor_tensor(dst, da_t1, da_t2, ALU.add).then_inc(da.da_roped, 1)
                        dve.wait_ge(da.da_roped, 2 * kk + 2)
                for gg in range(PERQ):
                    nc.vector.tensor_scalar(da_kTm[:, gg, :], da_kT, w.row_mask[:, gg:gg + 1], None,
                                            ALU.mult).then_inc(da.da_kt_kept, 1)
            dve.wait_ge(da.da_v_kept, k + 1)
            for gg in range(PERQ):
                nc.vector.tensor_tensor(da_Vm[:, gg, :, :], da_V, under(w.col_of[:, gg, :], [P, TILES, P]),
                                        ALU.mult).then_inc(da.da_vm_kept, 1)
            for qt in range(TILES):
                keys = (qt + 1) * P if causal else T
                for gg in range(PERQ):
                    i = PERQ * qt + gg
                    dve.wait_ge(da.da_scores_ready, A * k + i + 1)
                    nc.vector.tensor_reduce(mx[:, qt, gg:gg + 97:32], banks(4 * (i % 2), 4)[:, :, 0:keys], AX.X,
                                            ALU.max, negate=True).then_inc(da.da_max_kept, 1)
            dve.wait_ge(da.da_pv_done, A * k + A)
            nc.vector.reciprocal(da_inv, bank(7)).then_inc(da.da_inv_kept, 1)
            dve.wait_ge(da.da_inv_kept, k + 1)
            nc.vector.tensor_tensor(da_y, bank(6), da_inv, ALU.mult).then_inc(da.da_y_ready, 1)
            dve.wait_ge(da.da_out_ready, k + 1)
            if causal:
                last = nc.vector.tensor_tensor(x[:, unit(b)], bank(1), x[:, unit(b)], ALU.add)
            else:
                last = nc.vector.scalar_tensor_tensor(x[:, unit(b)], bank(1), w.ra_bo[:, 0:1], x[:, unit(b)], ALU.add, ALU.add)
            last.then_inc(g.unit_done, 1)
            dve.wait_ge(g.unit_done, u + 1)

        fo = sems("fo_proj_ready fo_kept fo_floor fo_exped fo_ready fo_step fo_prod fo_sum_ready fo_y_ready fo_out_ready")
        top[0] = 0
        fo_b = new(2, T)
        fo_e = new(2, T)
        fo_phi = [new(NB * T), new(NB * T)]
        fo_v, fo_f = new(NB * T), new(NB * T)
        fo_pr = new(2, T)
        fo_w = new(T)
        fo_decay = [new(T) for _ in range(NB)]
        fo_num, fo_den, fo_t, fo_y = new(T), new(T), new(T), new(T)
        FO_PAIRS = [(s, r) for s in range(NB) for r in range(s, -1, -1)]

        def forget_in_pe(pe, u, n, k, b):
            pe.wait_ge(g.unit_done, u)
            ln_pe(pe, n, x[:, unit(b)])
            pe.wait_ge(ln.ln_normed, n + 1)
            for i, wt in enumerate((w.fo_wq, w.fo_wk, w.fo_wv, w.fo_wf)):
                nc.tensor.matmul(bank(i), wt[:, :], xn_now, start=True, stop=True).then_inc(fo.fo_proj_ready, 1)

        def forget_in_act(act, u, n, k, b):
            ln_act(act, n)
            for i, bias in enumerate((w.fo_bq, w.fo_bk)):
                act.wait_ge(fo.fo_proj_ready, 4 * k + i + 1)
                nc.scalar.activation(fo_b[:, i, :], bank(i), ACT.Identity, bias=bias[:, :]).then_inc(fo.fo_kept, 1)
            act.wait_ge(fo.fo_proj_ready, 4 * k + 3)
            nc.scalar.activation(fo_v[:, unit(b)], bank(2), ACT.Identity, bias=w.fo_bv[:, :]).then_inc(fo.fo_ready, 1)
            act.wait_ge(fo.fo_floor, k + 1)
            nc.scalar.activation(fo_e, fo_e, ACT.Exp).then_inc(fo.fo_exped, 1)
            act.wait_ge(fo.fo_proj_ready, 4 * k + 4)
            nc.scalar.activation(fo_f[:, unit(b)], bank(3), ACT.Sigmoid, bias=w.fo_bf[:, :]).then_inc(fo.fo_ready, 1)

        def forget_in_dve(dve, u, n, k, b):
            ln_dve(dve, n, x[:, unit(b)], xn_now)
            dve.wait_ge(fo.fo_kept, 2 * k + 2)
            nc.vector.tensor_scalar(fo_e, fo_b, 0.0, None, ALU.min).then_inc(fo.fo_floor, 1)
            dve.wait_ge(fo.fo_exped, k + 1)
            for i in range(2):
                nc.vector.scalar_tensor_tensor(fo_phi[i][:, unit(b)], fo_b[:, i, :], 0.0, fo_e[:, i, :], ALU.max,
                                               ALU.add).then_inc(fo2.fo_phi_ready, 1)
            dve.wait_ge(fo2.fo_phi_ready, 2 * k + 2)
            dve.wait_ge(fo.fo_ready, 2 * k + 2)
            nc.vector.tensor_copy(fo_w[:, 0:1], fo_f[:, 0:1]).then_inc(g.unit_done, 1)
            dve.wait_ge(g.unit_done, u + 1)

        fo2 = sems("fo_phi_ready")

        def forget_out_pe(pe, u):
            for i, (s, r) in enumerate(FO_PAIRS):
                pe.wait_ge(fo.fo_prod, i + 1)
                if i >= 2:
                    pe.wait_ge(fo2b.fo_used, i - 1)
                nc.tensor.matmul(bank(i % 2), w.head_ones[:, :], fo_pr[:, i % 2, :], start=True, stop=True).then_inc(fo.fo_sum_ready, 1)
                if r == 0:
                    pe.wait_ge(fo.fo_y_ready, s + 1)
                    nc.tensor.matmul(bank(2), w.fo_wo[:, :], fo_y, start=True, stop=True).then_inc(fo.fo_out_ready, 1)

        fo2b = sems("fo_used")

        def forget_out_dve(dve, u):
            step, steps = link(dve, fo.fo_step, 0)

            def at(a, s):
                return a[:, s * T:(s + 1) * T]
            for i, (s, r) in enumerate(FO_PAIRS):
                nc.vector.tensor_tensor(fo_pr[:, i % 2, :], at(fo_phi[0], s), at(fo_phi[1], r), ALU.mult).then_inc(fo.fo_prod, 1)
                dve.wait_ge(fo.fo_sum_ready, i + 1)
                if r == s:
                    step(nc.vector.tensor_copy(fo_den, bank(i % 2)))
                    nc.vector.tensor_tensor(fo_num, bank(i % 2), at(fo_v, s), ALU.mult).then_inc(fo2b.fo_used, 1)
                    dve.wait_ge(fo2b.fo_used, i + 1)
                else:
                    if r == s - 1:
                        step(nc.vector.tensor_copy(fo_decay[r], at(fo_f, s)))
                    else:
                        step(nc.vector.tensor_tensor(fo_decay[r], fo_decay[r], at(fo_f, s), ALU.mult))
                    nc.vector.tensor_tensor(fo_w, bank(i % 2), fo_decay[r], ALU.mult).then_inc(fo2b.fo_used, 1)
                    dve.wait_ge(fo2b.fo_used, i + 1)
                    step(nc.vector.tensor_tensor(fo_den, fo_den, fo_w, ALU.add))
                    step(nc.vector.tensor_tensor(fo_t, fo_w, at(fo_v, r), ALU.mult))
                    step(nc.vector.tensor_tensor(fo_num, fo_num, fo_t, ALU.add))
                if r == 0:
                    step(nc.vector.tensor_scalar(fo_den, fo_den, 1e-6, None, ALU.add))
                    step(nc.vector.reciprocal(fo_t, fo_den))
                    nc.vector.tensor_tensor(fo_y, fo_num, fo_t, ALU.mult).then_inc(fo.fo_y_ready, 1)
                    dve.wait_ge(fo.fo_out_ready, s + 1)
                    nc.vector.scalar_tensor_tensor(at(x, s), bank(2), w.fo_bo[:, 0:1], at(x, s), ALU.add,
                                                   ALU.add).then_inc(g.unit_done, 1)
                    dve.wait_ge(g.unit_done, u + s + 1)

        tm = sems("tm_step tm_mixed tm_k_ready tm_v_ready tm_r_ready tm_ek_kept tm_sr_kept tm_scanned tm_y_ready tm_out_ready")
        top[0] = 0
        tm_d, tm_in, tm_ek, tm_ekv, tm_sr = new(T), new(3, T), new(T), new(T), new(T)
        tm_num, tm_den, tm_inv, tm_y = new(T), new(T), new(T), new(T)
        TM_STEPS = 6

        def time_pe(pe, u, n, k, b):
            pe.wait_ge(g.unit_done, u)
            ln_pe(pe, n, x[:, unit(b)])
            for i, (wt, ready) in enumerate(((w.tm_wk, tm.tm_k_ready), (w.tm_wv, tm.tm_v_ready), (w.tm_wr, tm.tm_r_ready))):
                pe.wait_ge(tm.tm_mixed, 3 * k + i + 1)
                nc.tensor.matmul(bank(i), wt[:, :], tm_in[:, i, :], start=True, stop=True).then_inc(ready, 1)
            pe.wait_ge(tm.tm_y_ready, k + 1)
            nc.tensor.matmul(bank(3), w.tm_wo[:, :], tm_y, start=True, stop=True).then_inc(tm.tm_out_ready, 1)

        def time_act(act, u, n, k, b):
            ln_act(act, n)
            act.wait_ge(tm.tm_k_ready, k + 1)
            nc.scalar.activation(tm_ek, bank(0), ACT.Exp).then_inc(tm.tm_ek_kept, 1)
            act.wait_ge(tm.tm_r_ready, k + 1)
            nc.scalar.activation(tm_sr, bank(2), ACT.Sigmoid).then_inc(tm.tm_sr_kept, 1)

        def time_dve(dve, u, n, k, b):
            ln_dve(dve, n, x[:, unit(b)], xn_now)
            step, steps = link(dve, tm.tm_step, TM_STEPS * k)
            dve.wait_ge(ln.ln_normed, n + 1)
            step(nc.vector.tensor_tensor(tm_d, xn_now, xn_prev, ALU.subtract))
            for i, mu in enumerate((w.tm_mk, w.tm_mv, w.tm_mr)):
                nc.vector.scalar_tensor_tensor(tm_in[:, i, :], tm_d, mu[:, 0:1], xn_prev, ALU.mult, ALU.add).then_inc(tm.tm_mixed, 1)
            dve.wait_ge(tm.tm_ek_kept, k + 1)
            dve.wait_ge(tm.tm_v_ready, k + 1)
            step(nc.vector.tensor_tensor(tm_ekv, bank(1), tm_ek, ALU.mult))
            for i, src in enumerate((tm_ekv, tm_ek)):
                nc.vector.tensor_tensor_scan(state[:, i, 1:1 + T], ew[:, 0:1].broadcast_to([P, T]), src, 0.0, ALU.mult,
                                             ALU.add).then_inc(tm.tm_scanned, 1)
            dve.wait_ge(tm.tm_scanned, 2 * k + 2)
            nc.vector.scalar_tensor_tensor(tm_num, tm_ekv, eu[:, 0:1], state[:, 0, 0:T], ALU.mult, ALU.add).then_inc(tm2.tm_num_ready, 1)
            step(nc.vector.scalar_tensor_tensor(tm_den, tm_ek, eu[:, 0:1], state[:, 1, 0:T], ALU.mult, ALU.add))
            step(nc.vector.reciprocal(tm_inv, tm_den))
            dve.wait_ge(tm2.tm_num_ready, k + 1)
            step(nc.vector.tensor_tensor(tm_num, tm_num, tm_inv, ALU.mult))
            dve.wait_ge(tm.tm_sr_kept, k + 1)
            nc.vector.tensor_tensor(tm_y, tm_num, tm_sr, ALU.mult).then_inc(tm.tm_y_ready, 1)
            dve.wait_ge(tm.tm_out_ready, k + 1)
            step(nc.vector.tensor_copy(tm_d, bank(3)))
            nc.vector.tensor_tensor(x[:, unit(b)], tm_d, x[:, unit(b)], ALU.add).then_inc(g.unit_done, 1)
            dve.wait_ge(g.unit_done, u + 1)
            assert steps[0] == TM_STEPS

        tm2 = sems("tm_num_ready")

        de = sems("deep_loaded_even deep_loaded_odd deep_tabs_ready deep_shifted deep_qk_ready deep_qk_squared deep_rope_parts deep_step "
                  "deep_std_ready deep_summed deep_roped deep_turned deep_turn_kept deep_v_ready deep_v_kept "
                  "deep_scores_ready deep_masked deep_max deep_less_max deep_exped deep_row_sum deep_row_inv "
                  "deep_probs_ready deep_probs_turned deep_probs_kept deep_pv_done deep_o_kept deep_attn_ready "
                  "deep_attn_added deep_affine deep_ln_ready deep_gate_ready deep_a_ready deep_gelu_done deep_hidden_ready "
                  "deep_ffn_ready")
        deep_loaded = (de.deep_loaded_even, de.deep_loaded_odd)
        top[0] = 0
        tabs = new(4, TILES, LD)
        qT_start = top[0]
        qT = new(PAIRS, T)
        V_start = top[0]
        V = new(T // WIN, T)
        phase_start = top[0]
        qk_sq = new(2 * LHEADS, LD)
        roped = new(2 * LHEADS, LD)
        turned = new(2 * LHEADS, LD)
        phase_end = top[0]
        top[0] = phase_start
        probs = new(PAIRS, 2, 2 * WIN)
        probsT = new(2, T)
        oT = new(PAIRS, T)
        top[0] = max(top[0], phase_end)
        h_sum, h_clamped, h_std, h_inv = (new(2 * LHEADS) for _ in range(4))
        row_max, row_sum, row_inv = (new(LHEADS) for _ in range(3))
        attention_end = top[0]
        top[0] = qT_start
        dn = new(T)
        gelu, hidden = new(3, T), new(3, T)
        assert top[0] <= V_start
        top[0] = attention_end
        H2 = [P, 2 * LHEADS, LD]

        def deep_pe(pe, u, n, k, b, h):
            W = deep_w[h]
            wqkv = W.wqkv
            pe.wait_ge(g.unit_done, u)
            pe.wait_ge(de.deep_shifted, 2 * (2 * k) + 2)
            for t in range(TILES + 1):
                if t < TILES:
                    if t >= 1:
                        pe.wait_ge(de.deep_rope_parts, 4 * (TILES * k + t))
                    for c in range(4):
                        last = nc.tensor.matmul(bank(c), xs[:, WIN + t * P:WIN + (t + 1) * P], wqkv[:, c * 512:(c + 1) * 512],
                                                start=True, stop=True)
                    last.then_inc(de.deep_qk_ready, 1)
                for m in range(4):
                    if t < TILES:
                        wi = WPT * t + m
                        if wi >= 2:
                            pe.wait_ge(de.deep_v_kept, T // WIN * k + wi - 1)
                        vw = wqkv[:, 2 * INNER:3 * INNER].rearrange("c (p r d) -> c r p d", r=2, d=LD)
                        for r in range(2):
                            last = nc.tensor.matmul(bank(4 + wi % 2)[64 * r:64 * r + 64, :], xs[:, WIN * wi:WIN * wi + 2 * WIN],
                                                    vw[:, r, :, :], start=True, stop=True)
                        last.then_inc(de.deep_v_ready, 1)
                    if t >= 1:
                        i = 4 * (t - 1) + m
                        if m == 0:
                            pe.wait_ge(de.deep_roped, TILES * k + t)
                        if i >= 2:
                            pe.wait_ge(de.deep_turn_kept, 4 * TILES * k + i - 1)
                        for c in range(4):
                            pair = 4 * m + c
                            last = nc.tensor.matmul(bank(6 + i % 2)[:, c * P:(c + 1) * P],
                                                    roped[:, 2 * pair:2 * pair + 2, :], w.ident[:, :], start=True, stop=True)
                        last.then_inc(de.deep_turned, 1)
            pe.wait_ge(de.deep_turn_kept, 4 * TILES * (k + 1))
            pe.wait_ge(de.deep_v_kept, T // WIN * (k + 1))
            for t in range(TILES + 1):
                if t < TILES:
                    if t >= 2:
                        pe.wait_ge(de.deep_masked, 2 * (TILES * k + t - 1))
                    apart(pe)
                    for pair in range(PAIRS):
                        for j in range(WPT):
                            for r in range(2):
                                r64, wi = slice(64 * r, 64 * r + 64), WPT * t + j
                                last = nc.tensor.matmul(bank(2 * (t % 2) + r)[32 * j:32 * j + 32, pair * 64:pair * 64 + 64],
                                                        qT[r64, pair, wi * WIN:(wi + 1) * WIN],
                                                        deep_kT[r64, pair, wi * WIN:(wi + 2) * WIN], start=True, stop=True)
                    last.then_inc(de.deep_scores_ready, 1)
                if t >= 1:
                    m = t - 1
                    pe.wait_ge(de.deep_probs_ready, TILES * k + m + 1)
                    for half in range(2):
                        if m >= 1:
                            pe.wait_ge(de.deep_probs_kept, 2 * (TILES * k + m - 1) + half + 1)
                        for c in range(4):
                            last = nc.tensor.matmul(bank(4 + half)[:, c * P:(c + 1) * P], probs[:, 4 * half + c, :, :],
                                                    w.ident[:, :], start=True, stop=True)
                        last.then_inc(de.deep_probs_turned, 1)
                    for half in range(2):
                        pe.wait_ge(de.deep_probs_kept, 2 * (TILES * k + m) + half + 1)
                        if m >= 1:
                            pe.wait_ge(de.deep_o_kept, 2 * (TILES * k + m - 1) + half + 1)
                        apart(pe)
                        for c in range(4):
                            pair = 4 * half + c
                            for j in range(WPT):
                                for r in range(2):
                                    r64 = slice(64 * r, 64 * r + 64)
                                    col = c * P + j * WIN
                                    last = nc.tensor.matmul(bank(6 + half)[r64, col:col + WIN],
                                                            V[r64, WPT * m + j, pair * 64:pair * 64 + 64],
                                                            probsT[r64, half, col:col + WIN], start=True, stop=True)
                        last.then_inc(de.deep_pv_done, 1)
            pe.wait_ge(de.deep_o_kept, 2 * TILES * (k + 1))
            for pair in range(PAIRS):
                last = nc.tensor.matmul(bank(0), W.wo[:, pair, :], oT[:, pair, :], start=(pair == 0), stop=(pair == PAIRS - 1))
            last.then_inc(de.deep_attn_ready, 1)
            pe.wait_ge(de.deep_shifted, 2 * (2 * k + 1) + 2)
            ln_pe(pe, n, xs_now)
            pe.wait_ge(de.deep_ln_ready, k + 1)
            for j, (c0, m) in enumerate(DIB):
                nc.tensor.matmul(bank(j)[0:m, :], W.w1[:, DI + c0:DI + c0 + m], dn, start=True, stop=True).then_inc(de.deep_gate_ready, 1)
            for j, (c0, m) in enumerate(DIB):
                nc.tensor.matmul(bank(5 + j)[0:m, :], W.w1[:, c0:c0 + m], dn, start=True, stop=True).then_inc(de.deep_a_ready, 1)
            for j, (c0, m) in enumerate(DIB):
                pe.wait_ge(de.deep_hidden_ready, 3 * k + j + 1)
                last = nc.tensor.matmul(bank(3), W.w2[0:m, j, :], hidden[0:m, j, :], start=(j == 0), stop=(j == 2))
            last.then_inc(de.deep_ffn_ready, 1)

        def deep_act(act, u, n, k, b, h):
            W = deep_w[h]
            act.wait_ge(g.unit_done, u)
            for t in range(TILES + 1):
                if t < TILES:
                    act.wait_ge(de.deep_qk_ready, TILES * k + t + 1)
                    if t >= 1:
                        act.wait_ge(de2.deep_sq_summed, TILES * k + t)
                    for s in range(2):
                        nc.scalar.activation(qk_sq[:, LHEADS * s:LHEADS * (s + 1), :],
                                             psum[:, 1024 * s:1024 * (s + 1)].rearrange("p (h d) -> p h d", d=LD),
                                             ACT.Square).then_inc(de.deep_qk_squared, 1)
                for m in range(4):
                    if t < TILES:
                        wi = WPT * t + m
                        act.wait_ge(de.deep_v_ready, T // WIN * k + wi + 1)
                        nc.scalar.activation(V[:, wi, :], bank(4 + wi % 2), ACT.Copy).then_inc(de.deep_v_kept, 1)
                    if m == 1 and t < TILES:
                        act.wait_ge(de2.deep_clamped, TILES * k + t + 1)
                        nc.scalar.activation(h_std, h_clamped, ACT.Sqrt).then_inc(de.deep_std_ready, 1)
                    if t >= 1:
                        i = 4 * (t - 1) + m
                        act.wait_ge(de.deep_turned, 4 * TILES * k + i + 1)
                        src = bank(6 + i % 2).rearrange("p (c t) -> p c t", t=P)
                        c0, tok = 4 * (m % 2), (t - 1) * P
                        dst = qT[:, c0:c0 + 4, tok:tok + P] if m < 2 else deep_kT[:, c0:c0 + 4, WIN + tok:WIN + tok + P]
                        nc.scalar.activation(dst, src, ACT.Copy).then_inc(de.deep_turn_kept, 1)
            for t in range(TILES):
                act.wait_ge(de.deep_less_max, TILES * k + t + 1)
                nc.scalar.activation(probs, probs, ACT.Exp).then_inc(de.deep_exped, 1)
                for half in range(2):
                    act.wait_ge(de.deep_probs_turned, 2 * (TILES * k + t) + half + 1)
                    if t >= 1:
                        act.wait_ge(de.deep_pv_done, 2 * (TILES * k + t - 1) + half + 1)
                    nc.scalar.activation(probsT[:, half, :], bank(4 + half), ACT.Copy).then_inc(de.deep_probs_kept, 1)
                for half in range(2):
                    act.wait_ge(de.deep_pv_done, 2 * (TILES * k + t) + half + 1)
                    nc.scalar.activation(oT[:, 4 * half:4 * half + 4, t * P:(t + 1) * P],
                                         bank(6 + half).rearrange("p (c t) -> p c t", t=P), ACT.Copy).then_inc(de.deep_o_kept, 1)
            ln_act(act, n)
            act.wait_ge(ln.ln_normed, n + 1)
            nc.scalar.activation(dn, dn, ACT.Identity, bias=W.vec[:, 1:2], scale=W.vec[:, 0:1]).then_inc(de.deep_ln_ready, 1)
            for j, (c0, m) in enumerate(DIB):
                act.wait_ge(de.deep_gate_ready, 3 * k + j + 1)
                nc.scalar.activation(gelu[0:m, j, :], bank(j)[0:m, :], ACT.Gelu, bias=W.vec[0:m, 6 + j:7 + j]).then_inc(de.deep_gelu_done, 1)

        def deep_dve(dve, u, n, k, b, h):
            W = deep_w[h]
            zb = b * T

            def shift(i):
                apart(dve)
                nc.vector.tensor_copy(xs[0:64, WIN:WIN + T], z[0:64, bass.ds(zb, T)]).then_inc(de.deep_shifted, 1)
                nc.vector.tensor_copy(xs[64:P, WIN + 1:WIN + T], z[64:P, bass.ds(zb, T - 1)]).then_inc(de.deep_shifted, 1)
                dve.wait_ge(de.deep_shifted, 2 * (2 * k + i) + 2)
            shift(0)
            nc.vector.tensor_tensor(tabs, w.rope64[:, :, :, :],
                                    W.scales.rearrange("p (a o) d -> p a o d", o=1).broadcast_to([P, 4, TILES, LD]),
                                    ALU.mult).then_inc(de.deep_tabs_ready, 1)
            dve.wait_ge(de.deep_tabs_ready, k + 1)
            qk = psum[:, 0:2048].rearrange("p (s h d) -> p s h d", s=2, d=LD)
            for t in range(TILES):
                i = TILES * k + t
                dve.wait_ge(de.deep_qk_squared, 2 * i + 2)
                nc.vector.tensor_reduce(h_sum, qk_sq, AX.X, ALU.add).then_inc(de2.deep_sq_summed, 1)
                dve.wait_ge(de2.deep_sq_summed, i + 1)
                nc.vector.tensor_scalar(h_clamped, h_sum, NORM_FLOOR, None, ALU.max).then_inc(de2.deep_clamped, 1)
                if t >= 1:
                    dve.wait_ge(de.deep_turned, 4 * i)
                for s in range(2):
                    hs = slice(LHEADS * s, LHEADS * (s + 1))
                    shape = [P, LHEADS, LD]
                    nc.vector.tensor_tensor(roped[:, hs, :], qk[:, s], under(tabs[:, 2 * s, t, :], shape),
                                            ALU.mult).then_inc(de.deep_rope_parts, 1)
                    swapped = qk[:, s].rearrange("p h (a e) -> p h a e", a=2)[:, :, ::-1, :]
                    sin = tabs[:, 2 * s + 1, t, :].rearrange("p (o a e) -> p o a e", o=1, a=2).broadcast_to([P, LHEADS, 2, LD // 2])
                    nc.vector.tensor_tensor(turned[:, hs, :].rearrange("p h (a e) -> p h a e", a=2), swapped, sin,
                                            ALU.mult).then_inc(de.deep_rope_parts, 1)
                dve.wait_ge(de.deep_rope_parts, 4 * (i + 1))
                nc.vector.tensor_tensor(roped, roped, turned, ALU.add).then_inc(de.deep_summed, 1)
                dve.wait_ge(de.deep_std_ready, i + 1)
                nc.vector.reciprocal(h_inv, h_std).then_inc(de.deep_step, 1)
                dve.wait_ge(de.deep_step, i + 1)
                dve.wait_ge(de.deep_summed, i + 1)
                nc.vector.tensor_tensor(roped, roped, over(h_inv, H2), ALU.mult).then_inc(de.deep_roped, 1)
            R = [P, LHEADS, 2 * WIN]
            flat = probs.rearrange("p a r c -> p (a r) c")
            for t in range(TILES):
                i = TILES * k + t
                mask = w.win_mask[:, 1 if t else 0, :]
                dve.wait_ge(de.deep_scores_ready, i + 1)
                if t >= 1:
                    dve.wait_ge(de.deep_probs_turned, 2 * i)
                for r in range(2):
                    nc.vector.tensor_tensor(probs[:, :, r, :], bank(2 * (t % 2) + r).rearrange("p (a c) -> p a c", c=64),
                                            under(mask, [P, PAIRS, 2 * WIN]), ALU.add).then_inc(de.deep_masked, 1)
                dve.wait_ge(de.deep_masked, 2 * (i + 1))
                nc.vector.tensor_reduce(row_max, flat, AX.X, ALU.max).then_inc(de.deep_max, 1)
                dve.wait_ge(de.deep_max, i + 1)
                nc.vector.tensor_tensor(flat, flat, over(row_max, R), ALU.subtract).then_inc(de.deep_less_max, 1)
                dve.wait_ge(de.deep_exped, i + 1)
                nc.vector.tensor_reduce(row_sum, flat, AX.X, ALU.add).then_inc(de.deep_row_sum, 1)
                dve.wait_ge(de.deep_row_sum, i + 1)
                nc.vector.reciprocal(row_inv, row_sum).then_inc(de.deep_row_inv, 1)
                dve.wait_ge(de.deep_row_inv, i + 1)
                nc.vector.tensor_tensor(flat, flat, over(row_inv, R), ALU.mult).then_inc(de.deep_probs_ready, 1)
            zu = z[:, bass.ds(zb, T)]
            dve.wait_ge(de.deep_attn_ready, k + 1)
            nc.vector.tensor_tensor(zu, bank(0), zu, ALU.add).then_inc(de.deep_attn_added, 1)
            dve.wait_ge(de.deep_attn_added, k + 1)
            shift(1)
            ln_dve(dve, n, xs_now, dn)
            for j, (c0, m) in enumerate(DIB):
                dve.wait_ge(de.deep_gelu_done, 3 * k + j + 1)
                dve.wait_ge(de.deep_a_ready, 3 * k + j + 1)
                nc.vector.scalar_tensor_tensor(hidden[0:m, j, :], bank(5 + j)[0:m, :], W.vec[0:m, 3 + j:4 + j], gelu[0:m, j, :],
                                               ALU.add, ALU.mult).then_inc(de.deep_hidden_ready, 1)
            dve.wait_ge(de.deep_ffn_ready, k + 1)
            nc.vector.scalar_tensor_tensor(zu, bank(3), W.vec[:, 2:3], zu, ALU.add, ALU.add).then_inc(g.unit_done, 1)
            dve.wait_ge(g.unit_done, u + 1)

        de2 = sems("deep_sq_summed deep_clamped")

        tm3 = sems("tm_const")

        plan, units, norms, seen = [], 1, 0, {}
        for kind in sublayers:
            same = "dense" if kind in ("mqa", "rope") else kind
            plan.append((kind, units, norms, seen.get(same, 0), seen.get(same, 0) - seen.get("only " + kind, 0)))
            if kind == "deep":
                units, norms, many = units + NB + DEPTH * NB + 1, norms + NB + DEPTH * NB, DEPTH * NB
            elif kind == "forget":
                units, norms, many = units + 2 * NB, norms + NB, NB
            else:
                units, norms, many = units + NB, norms + NB, NB
            seen[same] = seen.get(same, 0) + many
            seen["only " + kind] = seen.get("only " + kind, 0) + many
        last_unit = units

        n_fixed = len(fixed)
        block = ctx.enter_context(nc.Block())

        def per_unit(eng, body, u, n, k, *more):
            with eng.Fori(0, NB) as b:
                body(eng, b + u, b + n, b + k, b, *more)

        def deep_pairs(eng, body, u, n, k):
            with eng.Fori(0, DEPTH // 2) as i:
                for h in range(2):
                    with eng.Fori(0, NB) as b:
                        m = i * (2 * NB) + b + h * NB
                        body(eng, m + u, m + n, m + k, b, h, i)

        @block.sync
        def _(sp):
            for b in range(NB):
                sp.dma_start(x[:, b * T:(b + 1) * T], d["x"][:, b * T:(b + 1) * T]).then_inc(g.x_loaded, 16)
            for name in fixed:
                dst = raw[name] if name in raw else kept[name]
                sp.dma_start(dst[tuple(slice(None) for _ in dst.shape)], d[name]).then_inc(g.weights_loaded, 16)
            calls = 0
            for kind, u, n, k, other in plan:
                if kind != "deep":
                    continue
                with sp.Fori(0, DEPTH // 2) as i:
                    for h in range(2):
                        free = u + NB + i * (2 * NB) + (h - 1) * NB
                        sp.wait_ge(g.unit_done, free)
                        for name in layered:
                            dst = deep_kept[h][name]
                            src = d[name][bass.ds(i * 2 + h, 1)]
                            if len(src.shape) == 3:
                                src = src.rearrange("l p a -> p (l a)")
                            else:
                                src = src.rearrange("l p a b -> p (l a) b")
                            sp.dma_start(dst[tuple(slice(None) for _ in dst.shape)], src).then_inc(deep_loaded[h], 16)
                calls += 1
            sp.wait_ge(g.unit_done, last_unit)
            sp.dma_start(out, x[:, :]).then_inc(g.stored, 16)
            sp.wait_ge(g.stored, 16)

        N_DEEP = 16 * len(layered)

        def deep_waits(eng, call, i, h):
            eng.wait_ge(deep_loaded[h], i * N_DEEP + (call * DEPTH // 2 + 1) * N_DEEP)

        @block.gpsimd
        def _(pool):
            nc.gpsimd.memset(xn[:, 0:1], 0.0).then_inc(g.pads_zeroed, 1)
            nc.gpsimd.memset(xs[:, 0:WIN + 1], 0.0).then_inc(g.pads_zeroed, 1)
            nc.gpsimd.memset(mx[:, :, :], 0.0).then_inc(g.pads_zeroed, 1)
            nc.gpsimd.memset(state[:, :, 0:1], 0.0).then_inc(g.pads_zeroed, 1)
            nc.gpsimd.memset(deep_kT[:, :, 0:WIN], 0.0).then_inc(g.pads_zeroed, 1)
            nc.gpsimd.memset(eps[:, :], LN_EPS).then_inc(g.pads_zeroed, 1)

        PADS = 6

        def ready(eng):
            eng.wait_ge(g.x_loaded, 16 * NB)
            eng.wait_ge(g.weights_loaded, 16 * n_fixed)
            eng.wait_ge(g.pads_zeroed, PADS)

        @block.tensor
        def _(pe):
            ready(pe)
            pe.wait_ge(g.weights_scaled, 5)
            call = 0
            for kind, u, n, k, other in plan:
                if kind == "moe":
                    per_unit(pe, moe_pe, u, n, k)
                elif kind == "chan":
                    per_unit(pe, chan_pe, u, n, k)
                elif kind == "swiglu":
                    per_unit(pe, swiglu_pe, u, n, k)
                elif kind in ("mqa", "rope"):
                    per_unit(pe, dense_pe, u, n, k, kind == "mqa", other)
                elif kind == "time":
                    per_unit(pe, time_pe, u, n, k)
                elif kind == "forget":
                    per_unit(pe, forget_in_pe, u, n, k)
                    forget_out_pe(pe, u + NB)
                elif kind == "deep":
                    with pe.Fori(0, NB) as b:
                        pe.wait_ge(g.unit_done, b + u)
                        ln_pe(pe, b + n, x[:, unit(b)])

                    def body(eng, u_, n_, k_, b, h, i):
                        deep_waits(eng, call, i, h)
                        deep_pe(eng, u_, n_, k_, b, h)
                    deep_pairs(pe, body, u + NB, n + NB, k)
                    call += 1

        @block.scalar
        def _(act):
            ready(act)
            nc.scalar.activation(eu[:, :], w.tm_first[:, :], ACT.Exp).then_inc(tm3.tm_const, 1)
            nc.scalar.activation(ew[:, :], w.tm_decay[:, :], ACT.Exp).then_inc(tm3.tm_const, 1)
            act.wait_ge(tm3.tm_const, 2)
            nc.scalar.activation(ew[:, :], ew[:, :], ACT.Exp, scale=-1.0).then_inc(tm3.tm_const, 1)
            call = 0
            for kind, u, n, k, other in plan:
                if kind == "moe":
                    per_unit(act, moe_act, u, n, k)
                elif kind == "chan":
                    per_unit(act, chan_act, u, n, k)
                elif kind == "swiglu":
                    per_unit(act, swiglu_act, u, n, k)
                elif kind in ("mqa", "rope"):
                    per_unit(act, dense_act, u, n, k, kind == "mqa", other)
                elif kind == "time":
                    per_unit(act, time_act, u, n, k)
                elif kind == "forget":
                    per_unit(act, forget_in_act, u, n, k)
                elif kind == "deep":
                    with act.Fori(0, NB) as b:
                        ln_act(act, b + n)

                    def body(eng, u_, n_, k_, b, h, i):
                        deep_waits(eng, call, i, h)
                        deep_act(eng, u_, n_, k_, b, h)
                    deep_pairs(act, body, u + NB, n + NB, k)
                    call += 1

        @block.vector
        def _(dve):
            ready(dve)
            for src, dst in ((raw["sw_gate"], gate_w), (raw["sw_up"], up_w), (raw["sw_down"], down_w)):
                whole = tuple(slice(None) for _ in dst.shape)
                done = g.unit_done if dst is down_w else g.weights_scaled
                nc.vector.tensor_scalar(dst[whole], src[whole], 1.0 / 127.0, None, ALU.mult).then_inc(done, 1)
            nc.vector.tensor_copy(later_key_q[:, :], raw["later_key_q"]).then_inc(g.weights_scaled, 1)
            nc.vector.tensor_copy(later_key_k[:, :], raw["later_key_k"]).then_inc(g.weights_scaled, 1)
            nc.vector.tensor_copy(identb[:, :], w.ident[:, :]).then_inc(g.weights_scaled, 1)
            dve.wait_ge(tm3.tm_const, 3)
            call = 0
            for kind, u, n, k, other in plan:
                if kind == "moe":
                    per_unit(dve, moe_dve, u, n, k)
                elif kind == "chan":
                    per_unit(dve, chan_dve, u, n, k)
                elif kind == "swiglu":
                    per_unit(dve, swiglu_dve, u, n, k)
                elif kind in ("mqa", "rope"):
                    per_unit(dve, dense_dve, u, n, k, kind == "mqa", other)
                elif kind == "time":
                    per_unit(dve, time_dve, u, n, k)
                elif kind == "forget":
                    per_unit(dve, forget_in_dve, u, n, k)
                    forget_out_dve(dve, u + NB)
                elif kind == "deep":
                    with dve.Fori(0, NB) as b:
                        ln_dve(dve, b + n, x[:, unit(b)], z[:, unit(b)])
                        dve.wait_ge(ln.ln_normed, b + (n + 1))
                        nc.vector.tensor_copy(h_sum[:, 0:1], rstd[:, 0:1]).then_inc(g.unit_done, 1)

                    def body(eng, u_, n_, k_, b, h, i):
                        deep_waits(eng, call, i, h)
                        deep_dve(eng, u_, n_, k_, b, h)
                    deep_pairs(dve, body, u + NB, n + NB, k)
                    nc.vector.scalar_tensor_tensor(x[:, :], z[:, :], 0.5, x[:, :], ALU.mult, ALU.add).then_inc(g.unit_done, 1)
                    dve.wait_ge(g.unit_done, u + NB + DEPTH * NB + 1)
                    call += 1


def constants(np):
    f = np.float32
    p = np.arange(P)
    c = {"ident": np.eye(P, dtype=f), "avg": np.full((P, P), 1.0 / P, f)}
    c["head_ones"] = (p[:, None] // HD8 == p[None, :] // HD8).astype(f)
    c["later_key_q"] = np.where(p[None, :] > p[:, None], -FAR, 0).astype(f)
    c["later_key_k"] = np.where(p[:, None] > p[None, :], -FAR, 0).astype(f)
    of = (p // HD8) % PERQ
    gg = np.arange(PERQ)
    c["row_mask"] = (of[:, None] == gg).astype(f)
    c["col_of"] = np.broadcast_to((gg[:, None] == of[None, :]).astype(f), (P, PERQ, P)).copy()
    c["row_of"] = np.broadcast_to((p[:, None] % 32 == gg)[:, :, None], (P, PERQ, P)).astype(f)
    rot = np.zeros((P, P), f)
    ev = p[::2]
    rot[ev + 1, ev] = -1.0
    rot[ev, ev + 1] = 1.0
    c["rot8"] = rot
    inv = (1.0 / f(10000.0) ** (np.arange(0, HD8, 2, dtype=f) / f(HD8))).astype(f)
    ang = np.arange(T, dtype=f)[None, :] * inv[(p % HD8) // 2][:, None]
    c["rope8"] = np.stack([np.cos(ang), np.sin(ang)], 1).astype(f)
    c["moe_order"] = np.broadcast_to(np.arange(EXPERTS, 0, -1, dtype=f), (P, EXPERTS)).copy()
    q, k = (p % WIN)[:, None], np.arange(2 * WIN)[None, :]
    band = (k >= q) & (k <= q + WIN)
    first = band & ((p[:, None] >= WIN) | (k >= WIN))
    c["win_mask"] = np.stack([np.where(first, 0, -FAR), np.where(band, 0, -FAR)], 1).astype(f)
    half = np.arange(0, LD, 2, dtype=f)
    t = np.arange(T, dtype=f)
    fr = t[:, None] * (1.0 / f(10000.0) ** (half / f(LD))).astype(f)[None, :]
    base = (half + f(0.4 * LD)) / f(1.4 * LD)
    sc = (base[None, :] ** ((t - T // 2) / f(WIN // 2))[:, None]).astype(f)
    fr, sc = np.concatenate([fr, fr], 1), np.concatenate([sc, sc], 1)
    sign = np.where(np.arange(LD) < LD // 2, -1.0, 1.0).astype(f)
    cos, sin = np.cos(fr).astype(f), np.sin(fr).astype(f) * sign
    tab = np.stack([cos * sc * 8, sin * sc * 8, cos / sc, sin / sc], 0).astype(f)
    c["rope64"] = np.ascontiguousarray(tab.reshape(4, TILES, P, LD).transpose(2, 0, 1, 3))
    return c


def laid_out(np, v):
    L = {}
    col = lambda a: a.reshape(P, 1)
    rows = lambda a: np.broadcast_to(a, (P,) + a.shape)
    L["x"] = v["L0_attn_x"].reshape(NB * T, P).T
    L["moe_wg"] = v["L0_ffn_Wg"]
    L["moe_bg"] = rows(v["L0_ffn_bg"])
    L["moe_we"] = v["L0_ffn_We"].transpose(2, 0, 1)
    L["moe_be"] = v["L0_ffn_be"]
    L["mqa_down"] = v["L0_attn_Wc_down"]
    L["mqa_q"] = v["L0_attn_Wq_up"]
    L["mqa_k"] = np.tile(v["L0_attn_Wkv_up"][:, :HD8], (1, HEADS8))
    L["mqa_v"] = np.tile(v["L0_attn_Wkv_up"][:, HD8:], (1, HEADS8))
    L["mqa_proj"] = v["L0_attn_Wc_proj"]
    for n in ("q", "k", "v", "o"):
        L["ra_w" + n] = v["L1_attn_W" + n].T
        L["fo_w" + n] = v["L2_attn_W" + n].T
        L["fo_b" + n] = col(v["L2_attn_b" + n])
        L["ra_b" + n] = rows(v["L1_attn_bv"]) if n == "v" else col(v["L1_attn_b" + n])
    L["fo_wf"] = np.repeat(v["L2_attn_Wf"].T, HD8, axis=1)
    L["fo_bf"] = col(np.repeat(v["L2_attn_bf"], HD8))
    for n in ("r", "k", "v"):
        L["cm_w" + n] = v["L1_ffn_W_" + n].T
    L["cm_mu_r"], L["cm_mu_k"] = col(v["L1_ffn_mu_r"]), col(v["L1_ffn_mu_k"])
    L["sw_gate"], L["sw_up"] = v["L2_ffn_w_gate"].T, v["L2_ffn_w_up"].T
    L["sw_down"] = v["L2_ffn_w_down"].T.reshape(HBLK, P, P).transpose(1, 0, 2)
    for n in ("k", "v", "r", "o"):
        L["tm_w" + n] = v["L3_attn_W" + n].T
    L["tm_decay"], L["tm_first"] = col(v["L3_attn_time_decay"]), col(v["L3_attn_time_first"])
    for n in ("k", "v", "r"):
        L["tm_m" + n] = col(v["L3_attn_time_mix_" + n])
    L["deep_wqkv"] = v["L3_ffn_Wqkv"]
    L["deep_wo"] = v["L3_ffn_Wo"].reshape(DEPTH, PAIRS, P, P).transpose(0, 2, 1, 3)
    L["deep_w1"] = v["L3_ffn_W1"]
    w2 = np.zeros((DEPTH, 3 * P, P), v["L3_ffn_W2"].dtype)
    w2[:, :DI] = v["L3_ffn_W2"]
    L["deep_w2"] = w2.reshape(DEPTH, 3, P, P).transpose(0, 2, 1, 3)
    b1 = np.zeros((DEPTH, 2, 3 * P), v["L3_ffn_b1"].dtype)
    b1[:, :, :DI] = v["L3_ffn_b1"].reshape(DEPTH, 2, DI)
    L["deep_vec"] = np.concatenate([v["L3_ffn_ln_g"][:, None], v["L3_ffn_ln_b"][:, None], v["L3_ffn_b2"][:, None],
                                    b1.reshape(DEPTH, 6, P)], 1).transpose(0, 2, 1)
    scales = []
    for n in ("q", "k"):
        s = v[f"L3_ffn_{n}_scale"]
        scales += [s, np.concatenate([s[:, LD // 2:], s[:, :LD // 2]], 1)]
    L["deep_scales"] = np.broadcast_to(np.stack(scales, 1)[:, None], (DEPTH, P, 4, LD))
    return L


def kernel(**inputs):
    import numpy as np
    import concourse.bacc as bacc
    from concourse.bass_utils import run_bass_kernel_spmd

    arrays = laid_out(np, {k: np.asarray(a) for k, a in inputs.items()})
    arrays.update(constants(np))
    nc = bacc.Bacc("TRN2", target_bir_lowering=False, num_devices=1)
    arrays = {k: np.ascontiguousarray(a) for k, a in arrays.items()}
    d = {k: nc.dram_tensor("in_" + k, a.shape, mybir.dt.from_np(a.dtype), kind="ExternalInput").ap()
         for k, a in arrays.items()}
    out = nc.dram_tensor("out_0_dram", (P, NB * T), F32, kind="ExternalOutput").ap()
    program(nc, d, out, SUBLAYERS)
    r = run_bass_kernel_spmd(nc, [{"in_" + k: a for k, a in arrays.items()}], core_ids=[0])
    return np.ascontiguousarray(r.results[0]["out_0_dram"].T).reshape(NB, T, P)
```

```python
from collections import namedtuple
from contextlib import ExitStack

import concourse.bass as bass
from concourse import mybir

F32 = mybir.dt.float32
BF16 = mybir.dt.bfloat16
I32 = mybir.dt.int32
ALU = mybir.AluOpType
ACT = mybir.ActivationFunctionType
AX = mybir.AxisListType

P = 128
NB, T = 4, 512
TILES = T // P
HEADS8, HD8 = 16, 8
QUADS = 4
EXPERTS = 8
HID = 384
HBLK = HID // P
DEPTH, LHEADS, LD, WIN = 6, 16, 64, 32
PAIRS = LHEADS // 2
INNER = LHEADS * LD
WPT = P // WIN
DI = 341
DIB = [(0, 128), (128, 128), (256, DI - 256)]
LN_EPS = 1e-5
NORM_FLOOR = 1e-24
FAR = 1e30


ARENA = 21200

SUBLAYERS = ["moe", "mqa", "moe", "chan", "rope", "chan", "swiglu", "forget", "swiglu", "deep", "time", "deep"]


def program(nc, d, out, sublayers):
    with ExitStack() as ctx:
        def sb(name, shape, dt=F32):
            return ctx.enter_context(nc.sbuf_tensor(name, shape, dt))

        psum = ctx.enter_context(nc.psum_tensor("psum", [P, 8 * 512], F32))

        def bank(i):
            return psum[:, i * 512:(i + 1) * 512]

        def banks(i, n):
            return psum[:, i * 512:(i + n) * 512].rearrange("p (n c) -> p n c", c=512)

        fixed = [n for n in d if n != "x" and not n.startswith("deep_")]
        passing = ["later_key_q", "later_key_k", "sw_gate", "sw_up", "sw_down"]
        kept = {n: sb("w_" + n, list(d[n].shape), d[n].dtype) for n in fixed if n not in passing}
        w = namedtuple("Weights", kept)(**kept)
        identb = sb("identb", [P, P], BF16)
        later_key_q = sb("later_key_q", [P, P], BF16)
        later_key_k = sb("later_key_k", [P, P], BF16)
        layered = [n for n in d if n.startswith("deep_")]
        deep_kept = [{n: sb(f"{n}_{h}", list(d[n].shape[1:])) for n in layered} for h in range(2)]
        deep_w = [namedtuple("Layer", [n[5:] for n in layered])(*deep_kept[h].values()) for h in range(2)]

        x = sb("x", [P, NB * T])
        z = sb("z", [P, NB * T])
        eps = sb("eps", [P, 1])
        xc = sb("xc", [P, T])
        xc_sq = sb("xc_sq", [P, T])
        std = sb("std", [P, TILES])
        rstd = sb("rstd", [P, TILES])
        xn = sb("xn", [P, 1 + T])
        xn_now, xn_prev = xn[:, 1:1 + T], xn[:, 0:T]
        xs = sb("xs", [P, WIN + T])
        xs_now = xs[:, WIN:WIN + T]
        mx = sb("mx", [P, TILES, P])
        deep_kT = sb("deep_kT", [P, PAIRS, WIN + T])
        ew = sb("ew", [P, 1])
        eu = sb("eu", [P, 1])
        gate_w = sb("gate_w", [P, HID])
        up_w = sb("up_w", [P, HID])
        down_w = sb("down_w", [P, HBLK, P])

        arena = sb("arena", [P, ARENA])
        top = [0]

        def new(*shape):
            size = 1
            for s in shape:
                size *= s
            a = arena[:, top[0]:top[0] + size]
            top[0] += size
            assert top[0] <= ARENA, top[0]
            if len(shape) == 2:
                a = a.rearrange("p (a b) -> p a b", b=shape[1])
            elif len(shape) == 3:
                a = a.rearrange("p (a b c) -> p a b c", b=shape[1], c=shape[2])
            return a

        raw = {n: new(*d[n].shape[1:]).bitcast(d[n].dtype) for n in passing}

        def apart(eng):
            eng.sem_inc(g.waits_passed, 1)

        def sems(names):
            names = names.split()
            return namedtuple("Semaphores", names)(*[ctx.enter_context(nc.semaphore(n)) for n in names])

        def link(eng, counter, base):
            n = [0]

            def step(ins):
                n[0] += 1
                ins.then_inc(counter, 1)
                eng.wait_ge(counter, base + n[0])
            return step, n

        g = sems("waits_passed weights_loaded x_loaded pads_zeroed weights_scaled unit_done stored")
        ln = sems("ln_mean_ready ln_centred ln_squared ln_var_ready ln_std_ready ln_rstd_ready ln_rstd_spread ln_normed")

        def unit(b):
            return bass.ds(b * T, T)

        def ln_pe_mean(pe, n, src, a):
            nc.tensor.matmul(bank(a), w.avg[:, :], src, start=True, stop=True).then_inc(ln.ln_mean_ready, 1)

        def ln_pe_var(pe, n, v):
            pe.wait_ge(ln.ln_squared, n + 1)
            for t in range(TILES):
                last = nc.tensor.matmul(bank(v)[:, t:t + 1], xc_sq[:, t * P:(t + 1) * P], w.avg[:, 0:1],
                                        start=True, stop=True)
            last.then_inc(ln.ln_var_ready, 1)

        def ln_pe_spread(pe, n, a):
            pe.wait_ge(ln.ln_rstd_ready, n + 1)
            for t in range(TILES):
                last = nc.tensor.matmul(bank(a)[:, t * P:(t + 1) * P], rstd[:, t:t + 1].broadcast_to([P, P]),
                                        w.ident[:, :], start=True, stop=True)
            last.then_inc(ln.ln_rstd_spread, 1)

        def ln_pe(pe, n, src):
            ln_pe_mean(pe, n, src, 4)
            ln_pe_var(pe, n, 5)
            ln_pe_spread(pe, n, 4)

        def ln_act_square(act, n):
            act.wait_ge(ln.ln_centred, n + 1)
            nc.scalar.activation(xc_sq[:, :], xc[:, :], ACT.Square).then_inc(ln.ln_squared, 1)

        def ln_act_std(act, n, v):
            act.wait_ge(ln.ln_var_ready, n + 1)
            nc.scalar.activation(std[:, :], bank(v)[:, 0:TILES], ACT.Sqrt, bias=eps[:, :]).then_inc(ln.ln_std_ready, 1)

        def ln_act(act, n):
            ln_act_square(act, n)
            ln_act_std(act, n, 5)

        def ln_dve_centre(dve, n, src, a):
            dve.wait_ge(ln.ln_mean_ready, n + 1)
            nc.vector.tensor_tensor(xc[:, :], src, bank(a), ALU.subtract).then_inc(ln.ln_centred, 1)

        def ln_dve_rstd(dve, n):
            dve.wait_ge(ln.ln_std_ready, n + 1)
            nc.vector.reciprocal(rstd[:, :], std[:, :]).then_inc(ln.ln_rstd_ready, 1)

        def ln_dve_scale(dve, n, dst, a):
            dve.wait_ge(ln.ln_rstd_spread, n + 1)
            dve.wait_ge(ln.ln_centred, n + 1)
            nc.vector.tensor_tensor(dst, xc[:, :], bank(a), ALU.mult).then_inc(ln.ln_normed, 1)

        def ln_dve(dve, n, src, dst):
            ln_dve_centre(dve, n, src, 4)
            ln_dve_rstd(dve, n)
            ln_dve_scale(dve, n, dst, 4)

        cm = sems("cm_step cm_mixed cm_r_ready cm_k_ready cm_r_done cm_relu_done cm_squared cm_v_ready")
        top[0] = 0
        cm_d, cm_r, cm_k, cm_gate, cm_relu, cm_sq, cm_out = (new(T) for _ in range(7))
        CM_STEPS = 2

        def chan_pe(pe, u, n, k, b):
            pe.wait_ge(g.unit_done, u)
            ln_pe(pe, n, x[:, unit(b)])
            pe.wait_ge(cm.cm_mixed, 2 * k + 2)
            nc.tensor.matmul(bank(0), w.cm_wr[:, :], cm_r, start=True, stop=True).then_inc(cm.cm_r_ready, 1)
            nc.tensor.matmul(bank(1), w.cm_wk[:, :], cm_k, start=True, stop=True).then_inc(cm.cm_k_ready, 1)
            pe.wait_ge(cm.cm_squared, k + 1)
            nc.tensor.matmul(bank(2), w.cm_wv[:, :], cm_sq, start=True, stop=True).then_inc(cm.cm_v_ready, 1)

        def chan_act(act, u, n, k, b):
            ln_act(act, n)
            act.wait_ge(cm.cm_r_ready, k + 1)
            nc.scalar.activation(cm_gate, bank(0), ACT.Sigmoid).then_inc(cm.cm_r_done, 1)
            act.wait_ge(cm.cm_k_ready, k + 1)
            nc.scalar.activation(cm_relu, bank(1), ACT.Relu).then_inc(cm.cm_relu_done, 1)

        def chan_dve(dve, u, n, k, b):
            ln_dve(dve, n, x[:, unit(b)], xn_now)
            step, steps = link(dve, cm.cm_step, CM_STEPS * k)
            dve.wait_ge(ln.ln_normed, n + 1)
            step(nc.vector.tensor_tensor(cm_d, xn_now, xn_prev, ALU.subtract))
            for mu, dst in ((w.cm_mu_r, cm_r), (w.cm_mu_k, cm_k)):
                nc.vector.scalar_tensor_tensor(dst, cm_d, mu[:, 0:1], xn_prev, ALU.mult, ALU.add).then_inc(cm.cm_mixed, 1)
            dve.wait_ge(cm.cm_relu_done, k + 1)
            nc.vector.tensor_tensor(cm_sq, cm_relu, cm_relu, ALU.mult).then_inc(cm.cm_squared, 1)
            dve.wait_ge(cm.cm_r_done, k + 1)
            dve.wait_ge(cm.cm_v_ready, k + 1)
            step(nc.vector.tensor_tensor(cm_out, bank(2), cm_gate, ALU.mult))
            nc.vector.scalar_tensor_tensor(x[:, unit(b)], cm_out, 0.5, x[:, unit(b)], ALU.mult, ALU.add).then_inc(g.unit_done, 1)
            dve.wait_ge(g.unit_done, u + 1)
            assert steps[0] == CM_STEPS

        sw = sems("sw_gate_ready sw_up_ready sw_silu_done sw_gated sw_down_ready")
        top[0] = 0
        sw_silu, sw_h = new(HBLK, T), new(HBLK, T)
        SW_UP = [3, 5, 6]

        def swiglu_pe(pe, u, n, k, b):
            pe.wait_ge(g.unit_done, u)
            ln_pe(pe, n, x[:, unit(b)])
            pe.wait_ge(ln.ln_normed, n + 1)
            for j in range(HBLK):
                nc.tensor.matmul(bank(j), gate_w[:, j * P:(j + 1) * P], xn_now, start=True, stop=True).then_inc(sw.sw_gate_ready, 1)
                nc.tensor.matmul(bank(SW_UP[j]), up_w[:, j * P:(j + 1) * P], xn_now, start=True, stop=True).then_inc(sw.sw_up_ready, 1)
            for j in range(HBLK):
                pe.wait_ge(sw.sw_gated, HBLK * k + j + 1)
                last = nc.tensor.matmul(bank(7), down_w[:, j, :], sw_h[:, j, :], start=(j == 0), stop=(j == HBLK - 1))
            last.then_inc(sw.sw_down_ready, 1)

        def swiglu_act(act, u, n, k, b):
            ln_act(act, n)
            for j in range(HBLK):
                act.wait_ge(sw.sw_gate_ready, HBLK * k + j + 1)
                nc.scalar.activation(sw_silu[:, j, :], bank(j), ACT.Silu).then_inc(sw.sw_silu_done, 1)

        def swiglu_dve(dve, u, n, k, b):
            ln_dve(dve, n, x[:, unit(b)], xn_now)
            for j in range(HBLK):
                dve.wait_ge(sw.sw_silu_done, HBLK * k + j + 1)
                dve.wait_ge(sw.sw_up_ready, HBLK * k + j + 1)
                nc.vector.tensor_tensor(sw_h[:, j, :], bank(SW_UP[j]), sw_silu[:, j, :], ALU.mult).then_inc(sw.sw_gated, 1)
            dve.wait_ge(sw.sw_down_ready, k + 1)
            nc.vector.scalar_tensor_tensor(x[:, unit(b)], bank(7), 0.5, x[:, unit(b)], ALU.mult, ALU.add).then_inc(g.unit_done, 1)
            dve.wait_ge(g.unit_done, u + 1)

        mo = sems("moe_logits_ready moe_step moe_shifted moe_exped moe_gates_ready moe_gates_turned moe_gates_kept "
                  "moe_experts_ready moe_weighted moe_summed moe_out_ready")
        top[0] = 0
        G = [P, TILES, EXPERTS]
        lo, eq, rank, one1, lo2, one2, ex, gates = (new(TILES, EXPERTS) for _ in range(8))
        m1, m2, r1, r2, gsum, ginv = (new(TILES) for _ in range(6))
        gatesT = new(T)
        moe_prod, moe_acc = new(EXPERTS, P), new(2, P)
        MOE_STEPS = 14

        def over(a, shape):
            return a.rearrange("p (n o) -> p n o", o=1).broadcast_to(shape)

        def under(a, shape):
            return a.rearrange("p (o c) -> p o c", o=1).broadcast_to(shape)

        def moe_pe(pe, u, n, k, b):
            pe.wait_ge(g.unit_done, u)
            ln_pe(pe, n, x[:, unit(b)])
            pe.wait_ge(ln.ln_normed, n + 1)
            for t in range(TILES):
                last = nc.tensor.matmul(bank(5)[:, t * EXPERTS:(t + 1) * EXPERTS], xn[:, 1 + t * P:1 + (t + 1) * P],
                                        w.moe_wg[:, :], start=True, stop=True)
            last.then_inc(mo.moe_logits_ready, 1)
            for t in range(TILES):
                a = 2 * (t % 2)
                if t >= 2:
                    pe.wait_ge(mo.moe_weighted, TILES * k + t - 1)
                for h in range(2):
                    last = nc.tensor.matmul(bank(a + h), xn[:, 1 + t * P:1 + (t + 1) * P],
                                            w.moe_we[:, 4 * h:4 * h + 4, :], start=True, stop=True)
                last.then_inc(mo.moe_experts_ready, 1)
                if t == 0:
                    pe.wait_ge(mo.moe_gates_ready, k + 1)
                    for tt in range(TILES):
                        last = nc.tensor.matmul(bank(6)[0:EXPERTS, tt * P:(tt + 1) * P], gates[:, tt, :], w.ident[:, :],
                                                start=True, stop=True)
                    last.then_inc(mo.moe_gates_turned, 1)
                    pe.wait_ge(mo.moe_gates_kept, k + 1)
                    nc.tensor.matmul(bank(7), w.moe_be[:, :], gatesT[0:EXPERTS, :], start=True, stop=False, skip_group_check=True)
                if t >= 1:
                    moe_turn(pe, k, t - 1)
            moe_turn(pe, k, TILES - 1)

        def moe_turn(pe, k, t):
            pe.wait_ge(mo.moe_summed, TILES * k + t + 1)
            last = nc.tensor.matmul(bank(7)[:, t * P:(t + 1) * P], moe_acc[:, t % 2, :], w.ident[:, :],
                                    start=False, stop=(t == TILES - 1), skip_group_check=True)
            last.then_inc(mo.moe_out_ready, 1)

        def moe_act(act, u, n, k, b):
            ln_act(act, n)
            act.wait_ge(mo.moe_shifted, k + 1)
            nc.scalar.activation(ex, lo2, ACT.Exp).then_inc(mo.moe_exped, 1)
            act.wait_ge(mo.moe_gates_turned, k + 1)
            nc.scalar.activation(gatesT[0:EXPERTS, :], bank(6)[0:EXPERTS, :], ACT.Copy).then_inc(mo.moe_gates_kept, 1)

        def moe_dve(dve, u, n, k, b):
            ln_dve(dve, n, x[:, unit(b)], xn_now)
            step, steps = link(dve, mo.moe_step, MOE_STEPS * k)
            dve.wait_ge(mo.moe_logits_ready, k + 1)
            step(nc.vector.tensor_tensor(lo, bank(5)[:, 0:TILES * EXPERTS].rearrange("p (t e) -> p t e", e=EXPERTS),
                                         under(w.moe_bg[:, :], G), ALU.add))
            step(nc.vector.tensor_reduce(m1, lo, AX.X, ALU.max))
            step(nc.vector.tensor_tensor(eq, lo, over(m1, G), ALU.is_equal))
            step(nc.vector.tensor_tensor(rank, eq, under(w.moe_order[:, :], G), ALU.mult))
            step(nc.vector.tensor_reduce(r1, rank, AX.X, ALU.max))
            step(nc.vector.tensor_tensor(one1, rank, over(r1, G), ALU.is_equal))
            step(nc.vector.scalar_tensor_tensor(lo2, one1, -FAR, lo, ALU.mult, ALU.add))
            step(nc.vector.tensor_reduce(m2, lo2, AX.X, ALU.max))
            step(nc.vector.tensor_tensor(eq, lo2, over(m2, G), ALU.is_equal))
            step(nc.vector.tensor_tensor(rank, eq, under(w.moe_order[:, :], G), ALU.mult))
            step(nc.vector.tensor_reduce(r2, rank, AX.X, ALU.max))
            nc.vector.tensor_tensor(lo2, lo, over(m1, G), ALU.subtract).then_inc(mo.moe_shifted, 1)
            step(nc.vector.tensor_tensor(one2, rank, over(r2, G), ALU.is_equal))
            step(nc.vector.tensor_tensor(one1, one1, one2, ALU.add))
            dve.wait_ge(mo.moe_exped, k + 1)
            nc.vector.tensor_tensor(ex, ex, one1, ALU.mult).then_inc(mo.moe_step, 1)
            dve.wait_ge(mo.moe_step, MOE_STEPS * k + MOE_STEPS)
            steps[0] += 1
            assert steps[0] == MOE_STEPS
            nc.vector.tensor_reduce(gsum, ex, AX.X, ALU.add).then_inc(mo2.moe_gsum, 1)
            dve.wait_ge(mo2.moe_gsum, k + 1)
            nc.vector.reciprocal(ginv, gsum).then_inc(mo2.moe_ginv, 1)
            dve.wait_ge(mo2.moe_ginv, k + 1)
            nc.vector.tensor_tensor(gates, ex, over(ginv, G), ALU.mult).then_inc(mo.moe_gates_ready, 1)
            dve.wait_ge(mo.moe_gates_ready, k + 1)
            for t in range(TILES):
                a = 2 * (t % 2)
                dve.wait_ge(mo.moe_experts_ready, TILES * k + t + 1)
                nc.vector.tensor_tensor(moe_prod, psum[:, a * 512:(a + 2) * 512].rearrange("p (e o) -> p e o", o=P),
                                        over(gates[:, t, :], [P, EXPERTS, P]), ALU.mult).then_inc(mo.moe_weighted, 1)
                dve.wait_ge(mo.moe_weighted, TILES * k + t + 1)
                if t >= 2:
                    dve.wait_ge(mo.moe_out_ready, TILES * k + t - 1)
                nc.vector.tensor_reduce(moe_acc[:, t % 2, :], moe_prod.rearrange("p e o -> p o e"), AX.X,
                                        ALU.add).then_inc(mo.moe_summed, 1)
                dve.wait_ge(mo.moe_summed, TILES * k + t + 1)
            dve.wait_ge(mo.moe_out_ready, TILES * k + TILES)
            nc.vector.scalar_tensor_tensor(x[:, unit(b)], bank(7), 0.5, x[:, unit(b)], ALU.mult, ALU.add).then_inc(g.unit_done, 1)
            dve.wait_ge(g.unit_done, u + 1)

        mo2 = sems("moe_gsum moe_ginv")

        da = sems("da_latent_ready da_latent_kept da_q_ready da_k_ready da_v_ready da_qb_kept da_kb_kept da_rot_ready "
                  "da_roped da_step da_q_kept da_k_copied da_kt_kept da_scores_ready da_max_kept da_vals_laid da_vals_kept "
                  "da_max_turned da_max_copied da_st_ready da_probs_ready da_pv_done da_den_kept da_inv_kept "
                  "da_y_half da_out_ready")
        HALF = HEADS8 // 2
        HROWS = (slice(0, P // 2), slice(P // 2, P))
        STEPS = TILES * HEADS8
        BUFS = 4
        LAG = 2
        SPREAD = TILES * P + HD8
        top[0] = 0
        da_kM = new(HEADS8, T)
        da_Vflat = new(HEADS8 * SPREAD)
        da_Vm = da_Vflat[:, 0:HEADS8 * TILES * P].rearrange("p (h t c) -> p h t c", t=TILES, c=P)
        da_own = da_Vflat.rearrange("p (h r) -> p h r", r=SPREAD)
        da_q = new(2, T)
        early = top[0]
        da_PT = new(BUFS, T)
        da_den, da_y = new(T), new(T)
        top[0] = early
        da_lat, da_qT, da_kb, da_kT, da_t1, da_t2 = new(T), new(T), new(T), new(T), new(T), new(T)

        def dense_pe(pe, u, n, k, b, causal, other):
            A = TILES * QUADS
            pe.wait_ge(g.unit_done, u)
            ln_pe(pe, n, x[:, unit(b)])
            pe.wait_ge(ln.ln_normed, n + 1)
            if causal:
                nc.tensor.matmul(bank(0)[0:64, :], w.mqa_down[:, :], xn_now, start=True, stop=True).then_inc(da.da_latent_ready, 1)
                pe.wait_ge(da.da_latent_kept, (k - other) + 1)
                src, wq, wk, wv = da_lat[0:64, :], w.mqa_q, w.mqa_k, w.mqa_v
            else:
                src, wq, wk, wv = xn_now, w.ra_wq, w.ra_wk, w.ra_wv
            nc.tensor.matmul(bank(1), wq[:, :], src, start=True, stop=True).then_inc(da.da_q_ready, 1)
            nc.tensor.matmul(bank(2), wk[:, :], src, start=True, stop=True).then_inc(da.da_k_ready, 1)
            for t in range(TILES):
                last = nc.tensor.matmul(bank(3)[:, t * P:(t + 1) * P], src[:, t * P:(t + 1) * P], wv[:, :], start=True, stop=True)
            last.then_inc(da.da_v_ready, 1)
            if not causal:
                pe.wait_ge(da.da_qb_kept, (k - other) + 1)
                nc.tensor.matmul(bank(6), w.rot8[:, :], da_qT, start=True, stop=True).then_inc(da.da_rot_ready, 1)
                pe.wait_ge(da.da_kb_kept, (k - other) + 1)
                nc.tensor.matmul(bank(7), w.rot8[:, :], da_kb, start=True, stop=True).then_inc(da.da_rot_ready, 1)
            pe.wait_ge(da.da_q_kept, 4 * k + 4)
            for qt in range(TILES):
                keys = (qt + 1) * P if causal else T
                for r in range(QUADS):
                    i = QUADS * qt + r
                    a = 4 * (i % 2)
                    if qt == 0:
                        pe.wait_ge(da.da_kt_kept, HEADS8 * k + 4 * r + 4)
                    if i == 0:
                        pe.wait_ge(da.da_vals_kept, TILES * k + TILES)
                    if i >= 2:
                        pe.wait_ge(da.da_max_kept, A * k + i - 1)
                    for j in range(QUADS):
                        h = 4 * r + j
                        last = nc.tensor.matmul(bank(a + j)[:, 0:keys], da_q[:, h // HALF, qt * P:(qt + 1) * P],
                                                da_kM[:, h, 0:keys], start=True, stop=not causal)
                        if causal:
                            last = nc.tensor.matmul(bank(a + j)[:, qt * P:keys], identb[:, :], later_key_q[:, :],
                                                    start=False, stop=True)
                    last.then_inc(da.da_scores_ready, 1)
            pe.wait_ge(da.da_max_kept, A * k + A)
            for qt in range(TILES):
                last = nc.tensor.matmul(bank(0)[:, qt * P:(qt + 1) * P], mx[:, qt, :], w.ident[:, :], start=True, stop=True)
            last.then_inc(da.da_max_turned, 1)
            pe.wait_ge(da.da_max_copied, 2 * k + 2)
            for m in range(STEPS + LAG):
                if m < STEPS:
                    kt, h = m // HEADS8, m % HEADS8
                    q0 = kt * P if causal else 0
                    a = bank(m % BUFS)
                    if m >= BUFS:
                        pe.wait_ge(da.da_probs_ready, STEPS * k + m - BUFS + 1)
                    last = nc.tensor.matmul(a[:, q0:T], da_kM[:, h, kt * P:(kt + 1) * P], da_q[:, h // HALF, q0:T],
                                            start=True, stop=not causal)
                    if causal:
                        last = nc.tensor.matmul(a[:, q0:q0 + P], identb[:, :], later_key_k[:, :], start=False, stop=True)
                    last.then_inc(da.da_st_ready, 1)
                if m >= LAG:
                    v = m - LAG
                    kt, h = v // HEADS8, v % HEADS8
                    q0 = kt * P if causal else 0
                    pe.wait_ge(da.da_probs_ready, STEPS * k + v + 1)
                    nc.tensor.matmul(bank(6 + h // HALF)[:, q0:T], da_Vm[:, h, kt, :], da_PT[:, v % BUFS, q0:T],
                                     start=(kt == 0 and h % HALF == 0), stop=(kt == TILES - 1 and h % HALF == HALF - 1),
                                     skip_group_check=True).then_inc(da.da_pv_done, 1)
            pe.wait_ge(da.da_y_half, 2 * k + 2)
            nc.tensor.matmul(bank(1), (w.mqa_proj if causal else w.ra_wo)[:, :], da_y, start=True,
                             stop=True).then_inc(da.da_out_ready, 1)

        def dense_act(act, u, n, k, b, causal, other):
            ln_act(act, n)
            if causal:
                act.wait_ge(da.da_latent_ready, (k - other) + 1)
                nc.scalar.activation(da_lat[0:64, :], bank(0)[0:64, :], ACT.Copy).then_inc(da.da_latent_kept, 1)
                act.wait_ge(da.da_q_ready, k + 1)
                for s in range(2):
                    nc.scalar.activation(da_q[HROWS[s], s, :], bank(1)[HROWS[s], :], ACT.Copy,
                                         scale=HD8 ** -0.5).then_inc(da.da_q_kept, 1)
                act.wait_ge(da.da_k_ready, k + 1)
                nc.scalar.activation(da_kT, bank(2), ACT.Copy).then_inc(da.da_k_copied, 1)
            else:
                act.wait_ge(da.da_q_ready, k + 1)
                nc.scalar.activation(da_qT, bank(1), ACT.Identity, bias=w.ra_bq[:, :]).then_inc(da.da_qb_kept, 1)
                act.wait_ge(da.da_k_ready, k + 1)
                nc.scalar.activation(da_kb, bank(2), ACT.Identity, bias=w.ra_bk[:, :]).then_inc(da.da_kb_kept, 1)
            act.wait_ge(da.da_max_turned, k + 1)
            for s in range(2):
                free = HROWS[1 - s]
                nc.scalar.activation(da_q[free, s, :], bank(0)[free, :], ACT.Copy).then_inc(da.da_max_copied, 1)
            for m in range(STEPS):
                q0 = (m // HEADS8) * P if causal else 0
                if m >= BUFS:
                    act.wait_ge(da.da_pv_done, STEPS * k + m - BUFS + 1)
                act.wait_ge(da.da_st_ready, STEPS * k + m + 1)
                nc.scalar.activation(da_PT[:, m % BUFS, q0:T], bank(m % BUFS)[:, q0:T], ACT.Exp).then_inc(da.da_probs_ready, 1)

        def dense_lay_values(dve, call):
            step = lambda ins: ins.then_inc(da.da_vals_laid, 1)
            step(nc.vector.memset(da_Vflat, 0.0))
            dve.wait_ge(da.da_vals_laid, 3 * call + 1)
            at = HALF * SPREAD - P // 2
            second = da_Vflat[:, at:at + HALF * SPREAD].rearrange("p (h r) -> p h r", r=SPREAD)
            for own, c in ((da_own[:, 0:HALF, :], P // 2), (second, 0)):
                ones = own[:, :, 0:TILES * P].rearrange("p h (t c) -> p h t c", c=P)[:, :, :, c:c + HD8]
                step(nc.vector.memset(ones, 1.0))
            dve.wait_ge(da.da_vals_laid, 3 * call + 3)

        def dense_dve(dve, u, n, k, b, causal, other):
            A = TILES * QUADS
            for s in range(2):
                nc.vector.memset(da_q[HROWS[1 - s], s, :], 0.0).then_inc(da.da_q_kept, 1)
            ln_dve(dve, n, x[:, unit(b)], xn_now)
            if causal:
                dve.wait_ge(da.da_k_copied, (k - other) + 1)
            else:
                kk = (k - other)
                cos, sin = w.rope8[:, 0, :], w.rope8[:, 1, :]
                for m, (kept, src) in enumerate(((da.da_qb_kept, da_qT), (da.da_kb_kept, da_kb))):
                    dve.wait_ge(kept, kk + 1)
                    nc.vector.tensor_tensor(da_t1, src, cos, ALU.mult).then_inc(da.da_step, 1)
                    dve.wait_ge(da.da_rot_ready, 2 * kk + m + 1)
                    nc.vector.tensor_tensor(da_t2, bank(6 + m), sin, ALU.mult).then_inc(da.da_step, 1)
                    dve.wait_ge(da.da_step, 4 * kk + 2 * m + 2)
                    if m == 0:
                        nc.vector.tensor_tensor(da_t1, da_t1, da_t2, ALU.add).then_inc(da.da_roped, 1)
                        dve.wait_ge(da.da_roped, 2 * kk + 1)
                        for s in range(2):
                            nc.vector.tensor_scalar(da_q[HROWS[s], s, :], da_t1[HROWS[s], :], HD8 ** -0.5, None,
                                                    ALU.mult).then_inc(da.da_q_kept, 1)
                        dve.wait_ge(da.da_q_kept, 4 * k + 4)
                    else:
                        nc.vector.tensor_tensor(da_kT, da_t1, da_t2, ALU.add).then_inc(da.da_roped, 1)
                        dve.wait_ge(da.da_roped, 2 * kk + 2)
            dve.wait_ge(da.da_v_ready, k + 1)
            for t in range(TILES):
                own = da_own[:, :, t * P:t * P + HD8]
                new_v = bank(3)[:, t * P:(t + 1) * P].rearrange("p (h c) -> p h c", c=HD8)
                if causal:
                    last = nc.vector.tensor_copy(own, new_v)
                else:
                    last = nc.vector.tensor_tensor(own, new_v, w.ra_bv[:, :].rearrange("p (h c) -> p h c", c=HD8), ALU.add)
                last.then_inc(da.da_vals_kept, 1)
            for h in range(HEADS8):
                nc.vector.tensor_scalar(da_kM[:, h, :], da_kT, w.row_mask[:, h:h + 1], w.max_row[:, h:h + 1],
                                        ALU.mult, ALU.add).then_inc(da.da_kt_kept, 1)
            for qt in range(TILES):
                keys = (qt + 1) * P if causal else T
                for r in range(QUADS):
                    i = QUADS * qt + r
                    c = 4 * (r % 2) + (P // 2 if r < 2 else 0)
                    dve.wait_ge(da.da_scores_ready, A * k + i + 1)
                    nc.vector.tensor_reduce(mx[:, qt, c:c + 4], banks(4 * (i % 2), 4)[:, :, 0:keys], AX.X,
                                            ALU.max, negate=True).then_inc(da.da_max_kept, 1)
            dve.wait_ge(da.da_pv_done, STEPS * k + STEPS)
            for s in range(2):
                nc.vector.tensor_copy(da_den[HROWS[s], :], bank(6 + s)[HROWS[1 - s], :]).then_inc(da.da_den_kept, 1)
            dve.wait_ge(da.da_den_kept, 2 * k + 2)
            nc.vector.reciprocal(da_den, da_den).then_inc(da.da_inv_kept, 1)
            dve.wait_ge(da.da_inv_kept, k + 1)
            for s in range(2):
                nc.vector.tensor_tensor(da_y[HROWS[s], :], bank(6 + s)[HROWS[s], :], da_den[HROWS[s], :],
                                        ALU.mult).then_inc(da.da_y_half, 1)
            dve.wait_ge(da.da_out_ready, k + 1)
            if causal:
                last = nc.vector.tensor_tensor(x[:, unit(b)], bank(1), x[:, unit(b)], ALU.add)
            else:
                last = nc.vector.scalar_tensor_tensor(x[:, unit(b)], bank(1), w.ra_bo[:, 0:1], x[:, unit(b)], ALU.add, ALU.add)
            last.then_inc(g.unit_done, 1)
            dve.wait_ge(g.unit_done, u + 1)

        fo = sems("fo_proj_ready fo_kept fo_floor fo_exped fo_ready fo_step fo_prod fo_sum_ready fo_y_ready fo_out_ready")
        top[0] = 0
        fo_b = new(2, T)
        fo_e = new(2, T)
        fo_phi = [new(NB * T), new(NB * T)]
        fo_v, fo_f = new(NB * T), new(NB * T)
        fo_pr = new(2, T)
        fo_w = new(T)
        fo_decay = [new(T) for _ in range(NB)]
        fo_num, fo_den, fo_t, fo_y = new(T), new(T), new(T), new(T)
        FO_PAIRS = [(s, r) for s in range(NB) for r in range(s, -1, -1)]

        def forget_in_pe(pe, u, n, k, b):
            pe.wait_ge(g.unit_done, u)
            ln_pe(pe, n, x[:, unit(b)])
            pe.wait_ge(ln.ln_normed, n + 1)
            for i, wt in enumerate((w.fo_wq, w.fo_wk, w.fo_wv, w.fo_wf)):
                nc.tensor.matmul(bank(i), wt[:, :], xn_now, start=True, stop=True).then_inc(fo.fo_proj_ready, 1)

        def forget_in_act(act, u, n, k, b):
            ln_act(act, n)
            for i, bias in enumerate((w.fo_bq, w.fo_bk)):
                act.wait_ge(fo.fo_proj_ready, 4 * k + i + 1)
                nc.scalar.activation(fo_b[:, i, :], bank(i), ACT.Identity, bias=bias[:, :]).then_inc(fo.fo_kept, 1)
            act.wait_ge(fo.fo_proj_ready, 4 * k + 3)
            nc.scalar.activation(fo_v[:, unit(b)], bank(2), ACT.Identity, bias=w.fo_bv[:, :]).then_inc(fo.fo_ready, 1)
            act.wait_ge(fo.fo_floor, k + 1)
            nc.scalar.activation(fo_e, fo_e, ACT.Exp).then_inc(fo.fo_exped, 1)
            act.wait_ge(fo.fo_proj_ready, 4 * k + 4)
            nc.scalar.activation(fo_f[:, unit(b)], bank(3), ACT.Sigmoid, bias=w.fo_bf[:, :]).then_inc(fo.fo_ready, 1)

        def forget_in_dve(dve, u, n, k, b):
            ln_dve(dve, n, x[:, unit(b)], xn_now)
            dve.wait_ge(fo.fo_kept, 2 * k + 2)
            nc.vector.tensor_scalar(fo_e, fo_b, 0.0, None, ALU.min).then_inc(fo.fo_floor, 1)
            dve.wait_ge(fo.fo_exped, k + 1)
            for i in range(2):
                nc.vector.scalar_tensor_tensor(fo_phi[i][:, unit(b)], fo_b[:, i, :], 0.0, fo_e[:, i, :], ALU.max,
                                               ALU.add).then_inc(fo2.fo_phi_ready, 1)
            dve.wait_ge(fo2.fo_phi_ready, 2 * k + 2)
            dve.wait_ge(fo.fo_ready, 2 * k + 2)
            nc.vector.tensor_copy(fo_w[:, 0:1], fo_f[:, 0:1]).then_inc(g.unit_done, 1)
            dve.wait_ge(g.unit_done, u + 1)

        fo2 = sems("fo_phi_ready")

        def forget_out_pe(pe, u):
            for i, (s, r) in enumerate(FO_PAIRS):
                pe.wait_ge(fo.fo_prod, i + 1)
                if i >= 2:
                    pe.wait_ge(fo2b.fo_used, i - 1)
                nc.tensor.matmul(bank(i % 2), w.head_ones[:, :], fo_pr[:, i % 2, :], start=True, stop=True).then_inc(fo.fo_sum_ready, 1)
                if r == 0:
                    pe.wait_ge(fo.fo_y_ready, s + 1)
                    nc.tensor.matmul(bank(2), w.fo_wo[:, :], fo_y, start=True, stop=True).then_inc(fo.fo_out_ready, 1)

        fo2b = sems("fo_used")

        def forget_out_dve(dve, u):
            step, steps = link(dve, fo.fo_step, 0)

            def at(a, s):
                return a[:, s * T:(s + 1) * T]
            for i, (s, r) in enumerate(FO_PAIRS):
                nc.vector.tensor_tensor(fo_pr[:, i % 2, :], at(fo_phi[0], s), at(fo_phi[1], r), ALU.mult).then_inc(fo.fo_prod, 1)
                dve.wait_ge(fo.fo_sum_ready, i + 1)
                if r == s:
                    step(nc.vector.tensor_copy(fo_den, bank(i % 2)))
                    nc.vector.tensor_tensor(fo_num, bank(i % 2), at(fo_v, s), ALU.mult).then_inc(fo2b.fo_used, 1)
                    dve.wait_ge(fo2b.fo_used, i + 1)
                else:
                    if r == s - 1:
                        step(nc.vector.tensor_copy(fo_decay[r], at(fo_f, s)))
                    else:
                        step(nc.vector.tensor_tensor(fo_decay[r], fo_decay[r], at(fo_f, s), ALU.mult))
                    nc.vector.tensor_tensor(fo_w, bank(i % 2), fo_decay[r], ALU.mult).then_inc(fo2b.fo_used, 1)
                    dve.wait_ge(fo2b.fo_used, i + 1)
                    step(nc.vector.tensor_tensor(fo_den, fo_den, fo_w, ALU.add))
                    step(nc.vector.tensor_tensor(fo_t, fo_w, at(fo_v, r), ALU.mult))
                    step(nc.vector.tensor_tensor(fo_num, fo_num, fo_t, ALU.add))
                if r == 0:
                    step(nc.vector.tensor_scalar(fo_den, fo_den, 1e-6, None, ALU.add))
                    step(nc.vector.reciprocal(fo_t, fo_den))
                    nc.vector.tensor_tensor(fo_y, fo_num, fo_t, ALU.mult).then_inc(fo.fo_y_ready, 1)
                    dve.wait_ge(fo.fo_out_ready, s + 1)
                    nc.vector.scalar_tensor_tensor(at(x, s), bank(2), w.fo_bo[:, 0:1], at(x, s), ALU.add,
                                                   ALU.add).then_inc(g.unit_done, 1)
                    dve.wait_ge(g.unit_done, u + s + 1)

        tm = sems("tm_step tm_mixed tm_k_ready tm_v_ready tm_r_ready tm_ek_kept tm_sr_kept tm_scanned tm_y_ready tm_out_ready")
        top[0] = 0
        tm_d, tm_in, tm_ek, tm_ekv, tm_sr = new(T), new(3, T), new(T), new(T), new(T)
        tm_num, tm_den, tm_inv, tm_y = new(T), new(T), new(T), new(T)
        state = new(2, 1 + T)
        TM_STEPS = 7

        def time_pe(pe, u, n, k, b):
            pe.wait_ge(g.unit_done, u)
            ln_pe(pe, n, x[:, unit(b)])
            for i, (wt, ready) in enumerate(((w.tm_wk, tm.tm_k_ready), (w.tm_wv, tm.tm_v_ready), (w.tm_wr, tm.tm_r_ready))):
                pe.wait_ge(tm.tm_mixed, 3 * k + i + 1)
                nc.tensor.matmul(bank(i), wt[:, :], tm_in[:, i, :], start=True, stop=True).then_inc(ready, 1)
            pe.wait_ge(tm.tm_y_ready, k + 1)
            nc.tensor.matmul(bank(3), w.tm_wo[:, :], tm_y, start=True, stop=True).then_inc(tm.tm_out_ready, 1)

        def time_act(act, u, n, k, b):
            ln_act(act, n)
            act.wait_ge(tm.tm_k_ready, k + 1)
            nc.scalar.activation(tm_ek, bank(0), ACT.Exp).then_inc(tm.tm_ek_kept, 1)
            act.wait_ge(tm.tm_r_ready, k + 1)
            nc.scalar.activation(tm_sr, bank(2), ACT.Sigmoid).then_inc(tm.tm_sr_kept, 1)

        def time_dve(dve, u, n, k, b):
            ln_dve(dve, n, x[:, unit(b)], xn_now)
            step, steps = link(dve, tm.tm_step, TM_STEPS * k)
            dve.wait_ge(ln.ln_normed, n + 1)
            step(nc.vector.tensor_tensor(tm_d, xn_now, xn_prev, ALU.subtract))
            for i, mu in enumerate((w.tm_mk, w.tm_mv, w.tm_mr)):
                nc.vector.scalar_tensor_tensor(tm_in[:, i, :], tm_d, mu[:, 0:1], xn_prev, ALU.mult, ALU.add).then_inc(tm.tm_mixed, 1)
            dve.wait_ge(tm.tm_ek_kept, k + 1)
            dve.wait_ge(tm.tm_v_ready, k + 1)
            step(nc.vector.tensor_tensor(tm_ekv, bank(1), tm_ek, ALU.mult))
            step(nc.vector.memset(state[:, :, 0:1], 0.0))
            for i, src in enumerate((tm_ekv, tm_ek)):
                nc.vector.tensor_tensor_scan(state[:, i, 1:1 + T], ew[:, 0:1].broadcast_to([P, T]), src, 0.0, ALU.mult,
                                             ALU.add).then_inc(tm.tm_scanned, 1)
            dve.wait_ge(tm.tm_scanned, 2 * k + 2)
            nc.vector.scalar_tensor_tensor(tm_num, tm_ekv, eu[:, 0:1], state[:, 0, 0:T], ALU.mult, ALU.add).then_inc(tm2.tm_num_ready, 1)
            step(nc.vector.scalar_tensor_tensor(tm_den, tm_ek, eu[:, 0:1], state[:, 1, 0:T], ALU.mult, ALU.add))
            step(nc.vector.reciprocal(tm_inv, tm_den))
            dve.wait_ge(tm2.tm_num_ready, k + 1)
            step(nc.vector.tensor_tensor(tm_num, tm_num, tm_inv, ALU.mult))
            dve.wait_ge(tm.tm_sr_kept, k + 1)
            nc.vector.tensor_tensor(tm_y, tm_num, tm_sr, ALU.mult).then_inc(tm.tm_y_ready, 1)
            dve.wait_ge(tm.tm_out_ready, k + 1)
            step(nc.vector.tensor_copy(tm_d, bank(3)))
            nc.vector.tensor_tensor(x[:, unit(b)], tm_d, x[:, unit(b)], ALU.add).then_inc(g.unit_done, 1)
            dve.wait_ge(g.unit_done, u + 1)
            assert steps[0] == TM_STEPS

        tm2 = sems("tm_num_ready")

        de = sems("deep_loaded_even deep_loaded_odd deep_tabs_ready deep_shifted deep_ffn_shifted deep_qk_ready deep_qk_squared deep_rope_parts deep_recip "
                  "deep_std_ready deep_summed deep_roped deep_turned deep_turn_kept deep_v_ready deep_v_kept "
                  "deep_scores_ready deep_masked deep_max deep_less_max deep_exped deep_row_sum deep_row_inv "
                  "deep_probs_ready deep_probs_turned deep_probs_kept deep_pv_done deep_o_kept deep_attn_ready "
                  "deep_attn_added deep_affine deep_ln_ready deep_gate_ready deep_a_ready deep_gelu_done deep_hidden_ready "
                  "deep_ffn_ready")
        deep_loaded = (de.deep_loaded_even, de.deep_loaded_odd)
        top[0] = 0
        tabs = new(4, TILES, LD)
        qT = new(PAIRS, T)
        V = new(T // WIN, T)
        phase_start = top[0]
        qk_sq = new(2 * LHEADS, LD)
        roped = new(2 * LHEADS, LD)
        turned = new(2 * LHEADS, LD)
        phase_end = top[0]
        top[0] = phase_start
        probs = new(PAIRS, 2, 2 * WIN)
        probsT = new(2, T)
        oT = new(PAIRS, T)
        top[0] = max(top[0], phase_end)
        h_sum, h_clamped, h_std, h_inv = (new(2 * LHEADS) for _ in range(4))
        row_max, row_sum, row_inv = (new(LHEADS) for _ in range(3))
        hidden = new(3, T)
        xf = xn[:, 0:T]
        dn = xc[:, :]
        gelu = xc_sq[:, :]
        H2 = [P, 2 * LHEADS, LD]

        def deep_ffn_pe(pe, piece, f):
            if f is None:
                return
            u, n, k, b, h = f
            W = deep_w[h]
            if piece == "mean":
                pe.wait_ge(de.deep_ffn_shifted, 2 * k + 2)
                ln_pe_mean(pe, n, xf, 6)
            elif piece == "var":
                ln_pe_var(pe, n, 7)
            elif piece == "spread":
                ln_pe_spread(pe, n, 6)
            elif piece == "down":
                pe.wait_ge(de.deep_gelu_done, 3 * k + 3)
                for j, (c0, m) in enumerate(DIB):
                    pe.wait_ge(de.deep_hidden_ready, 3 * k + j + 1)
                    last = nc.tensor.matmul(bank(6), W.w2[0:m, j, :], hidden[0:m, j, :], start=(j == 0), stop=(j == 2))
                last.then_inc(de.deep_ffn_ready, 1)
            else:
                j = piece
                c0, m = DIB[j]
                if j == 0:
                    pe.wait_ge(de.deep_ln_ready, k + 1)
                else:
                    pe.wait_ge(de.deep_gelu_done, 3 * k + j)
                nc.tensor.matmul(bank(6)[0:m, :], W.w1[:, DI + c0:DI + c0 + m], dn, start=True, stop=True).then_inc(de.deep_gate_ready, 1)
                if j > 0:
                    pe.wait_ge(de.deep_hidden_ready, 3 * k + j)
                nc.tensor.matmul(bank(7)[0:m, :], W.w1[:, c0:c0 + m], dn, start=True, stop=True).then_inc(de.deep_a_ready, 1)

        def deep_ffn_act(act, piece, f):
            if f is None:
                return
            u, n, k, b, h = f
            W = deep_w[h]
            if piece == "square":
                ln_act_square(act, n)
            elif piece == "std":
                ln_act_std(act, n, 7)
            elif piece == "affine":
                act.wait_ge(ln.ln_normed, n + 1)
                nc.scalar.activation(dn, dn, ACT.Identity, bias=W.vec[:, 1:2], scale=W.vec[:, 0:1]).then_inc(de.deep_ln_ready, 1)
            else:
                j = piece
                c0, m = DIB[j]
                act.wait_ge(de.deep_gate_ready, 3 * k + j + 1)
                if j > 0:
                    act.wait_ge(de.deep_hidden_ready, 3 * k + j)
                nc.scalar.activation(gelu[0:m, :], bank(6)[0:m, :], ACT.Gelu, bias=W.vec[0:m, 6 + j:7 + j]).then_inc(de.deep_gelu_done, 1)

        def deep_ffn_dve(dve, piece, f):
            if f is None:
                return
            u, n, k, b, h = f
            W = deep_w[h]
            zu = z[:, bass.ds(b * T, T)]
            if piece == "start":
                dve.wait_ge(de.deep_attn_ready, k + 1)
                nc.vector.tensor_tensor(zu, bank(6), zu, ALU.add).then_inc(de.deep_attn_added, 1)
                dve.wait_ge(de.deep_attn_added, k + 1)
                apart(dve)
                nc.vector.tensor_copy(xf[0:64, :], z[0:64, bass.ds(b * T, T)]).then_inc(de.deep_ffn_shifted, 1)
                nc.vector.tensor_copy(xf[64:P, 1:T], z[64:P, bass.ds(b * T, T - 1)]).then_inc(de.deep_ffn_shifted, 1)
                dve.wait_ge(de.deep_ffn_shifted, 2 * k + 2)
            elif piece == "centre":
                ln_dve_centre(dve, n, xf, 6)
            elif piece == "rstd":
                ln_dve_rstd(dve, n)
            elif piece == "scale":
                ln_dve_scale(dve, n, dn, 6)
            elif piece == "end":
                dve.wait_ge(de.deep_ffn_ready, k + 1)
                nc.vector.scalar_tensor_tensor(zu, bank(6), W.vec[:, 2:3], zu, ALU.add, ALU.add).then_inc(g.unit_done, 1)
            else:
                j = piece
                c0, m = DIB[j]
                dve.wait_ge(de.deep_gelu_done, 3 * k + j + 1)
                dve.wait_ge(de.deep_a_ready, 3 * k + j + 1)
                nc.vector.scalar_tensor_tensor(hidden[0:m, j, :], bank(7)[0:m, :], W.vec[0:m, 3 + j:4 + j], gelu[0:m, :],
                                               ALU.add, ALU.mult).then_inc(de.deep_hidden_ready, 1)

        V_LATER = [[8, 9, 10, 11], [12, 13], [14, 15], []]
        FFN_PE = ["mean", "var", "spread", 0, 1, 2, "down"]
        FFN_ACT = ["square", "std", "affine", 0, 1, 2]
        FFN_DVE = ["start", "centre", "rstd", "scale", 0, 1, 2, "end"]

        def deep_pe(pe, u, n, k, b, h, f):
            W = deep_w[h]
            wqkv = W.wqkv
            vw = wqkv[:, 2 * INNER:3 * INNER].rearrange("c (p r d) -> c r p d", r=2, d=LD)

            def v_of_window(wi, to):
                for r in range(2):
                    last = nc.tensor.matmul(bank(to)[64 * r:64 * r + 64, :], xs[:, WIN * wi:WIN * wi + 2 * WIN],
                                            vw[:, r, :, :], start=True, stop=True)
                last.then_inc(de.deep_v_ready, 1)
            pe.wait_ge(de.deep_shifted, 2 * k + 2)
            for t in range(TILES + 1):
                if t < TILES:
                    for s in range(2):
                        if t >= 1:
                            pe.wait_ge(de.deep_rope_parts, 4 * (TILES * k + t) - 2 + 2 * s)
                        for c in (2 * s, 2 * s + 1):
                            last = nc.tensor.matmul(bank(c), xs[:, WIN + t * P:WIN + (t + 1) * P],
                                                    wqkv[:, c * 512:(c + 1) * 512], start=True, stop=True)
                        last.then_inc(de.deep_qk_ready, 1)
                for m in range(4):
                    if t >= 1:
                        i = 4 * (t - 1) + m
                        if m == 0:
                            pe.wait_ge(de.deep_roped, TILES * k + t)
                        if m < 2:
                            pe.wait_ge(de.deep_v_kept, T // WIN * k + 2 * (t - 1) + m + 1)
                        else:
                            pe.wait_ge(de.deep_turn_kept, 4 * TILES * k + i - 1)
                        for c in range(4):
                            pair = 4 * m + c
                            last = nc.tensor.matmul(bank(4 + m % 2)[:, c * P:(c + 1) * P],
                                                    roped[:, 2 * pair:2 * pair + 2, :], w.ident[:, :], start=True, stop=True)
                        last.then_inc(de.deep_turned, 1)
                    if t == TILES and m >= 1:
                        deep_ffn_pe(pe, m - 1, f)
                if t < TILES:
                    for m in range(2):
                        if t >= 1:
                            pe.wait_ge(de.deep_turn_kept, 4 * TILES * k + 4 * (t - 1) + 3 + m)
                        v_of_window(2 * t + m, 4 + m)
                if t in (0, 2, 3):
                    deep_ffn_pe(pe, {0: "mean", 2: "var", 3: "spread"}[t], f)
            pe.wait_ge(de.deep_turn_kept, 4 * TILES * (k + 1))
            for t in range(TILES + 1):
                if t < TILES:
                    if t >= 1:
                        pe.wait_ge(de.deep_masked, 2 * (TILES * k + t))
                    apart(pe)
                    for pair in range(PAIRS):
                        for j in range(WPT):
                            for r in range(2):
                                r64, wi = slice(64 * r, 64 * r + 64), WPT * t + j
                                last = nc.tensor.matmul(bank(r)[32 * j:32 * j + 32, pair * 64:pair * 64 + 64],
                                                        qT[r64, pair, wi * WIN:(wi + 1) * WIN],
                                                        deep_kT[r64, pair, wi * WIN:(wi + 2) * WIN], start=True, stop=True)
                    last.then_inc(de.deep_scores_ready, 1)
                    if t == 0:
                        deep_ffn_pe(pe, "down", f)
                    for wi in V_LATER[t]:
                        if wi >= V_LATER[0][0] + 2:
                            pe.wait_ge(de.deep_v_kept, T // WIN * k + wi - 1)
                        v_of_window(wi, 2 + wi % 2)
                if t == TILES:
                    pe.wait_ge(de.deep_v_kept, T // WIN * (k + 1))
                if t >= 1:
                    m = t - 1
                    pe.wait_ge(de.deep_probs_ready, TILES * k + m + 1)
                    for half in range(2):
                        if m >= 1:
                            pe.wait_ge(de.deep_probs_kept, 2 * (TILES * k + m - 1) + half + 1)
                        for c in range(4):
                            last = nc.tensor.matmul(bank(4 + half)[:, c * P:(c + 1) * P], probs[:, 4 * half + c, :, :],
                                                    w.ident[:, :], start=True, stop=True)
                        last.then_inc(de.deep_probs_turned, 1)
                    pe.wait_ge(de.deep_v_kept, T // WIN * k + WPT * (m + 1))
                    for half in range(2):
                        pe.wait_ge(de.deep_probs_kept, 2 * (TILES * k + m) + half + 1)
                        if m >= 1:
                            pe.wait_ge(de.deep_o_kept, 2 * (TILES * k + m - 1) + half + 1)
                        apart(pe)
                        for c in range(4):
                            pair = 4 * half + c
                            for j in range(WPT):
                                for r in range(2):
                                    r64 = slice(64 * r, 64 * r + 64)
                                    col = c * P + j * WIN
                                    last = nc.tensor.matmul(bank(6 + half)[r64, col:col + WIN],
                                                            V[r64, WPT * m + j, pair * 64:pair * 64 + 64],
                                                            probsT[r64, half, col:col + WIN], start=True, stop=True)
                        last.then_inc(de.deep_pv_done, 1)
            pe.wait_ge(de.deep_o_kept, 2 * TILES * (k + 1))
            for pair in range(PAIRS):
                last = nc.tensor.matmul(bank(6), W.wo[:, pair, :], oT[:, pair, :], start=(pair == 0), stop=(pair == PAIRS - 1))
            last.then_inc(de.deep_attn_ready, 1)

        def deep_act(act, u, n, k, b, h, f):
            def keep_v(wi, at):
                act.wait_ge(de.deep_v_ready, T // WIN * k + wi + 1)
                nc.scalar.activation(V[:, wi, :], bank(at), ACT.Copy).then_inc(de.deep_v_kept, 1)
            for t in range(TILES + 1):
                if t < TILES:
                    if t >= 1:
                        act.wait_ge(de2.deep_sq_summed, TILES * k + t)
                    for s in range(2):
                        act.wait_ge(de.deep_qk_ready, 2 * (TILES * k + t) + s + 1)
                        nc.scalar.activation(qk_sq[:, LHEADS * s:LHEADS * (s + 1), :],
                                             psum[:, 1024 * s:1024 * (s + 1)].rearrange("p (h d) -> p h d", d=LD),
                                             ACT.Square).then_inc(de.deep_qk_squared, 1)
                else:
                    deep_ffn_act(act, "affine", f)
                for m in range(4):
                    if t >= 1:
                        i = 4 * (t - 1) + m
                        act.wait_ge(de.deep_turned, 4 * TILES * k + i + 1)
                        src = bank(4 + m % 2).rearrange("p (c t) -> p c t", t=P)
                        c0, tok = 4 * (m % 2), (t - 1) * P
                        dst = qT[:, c0:c0 + 4, tok:tok + P] if m < 2 else deep_kT[:, c0:c0 + 4, WIN + tok:WIN + tok + P]
                        nc.scalar.activation(dst, src, ACT.Copy).then_inc(de.deep_turn_kept, 1)
                    if t == TILES and m >= 1:
                        deep_ffn_act(act, m - 1, f)
                if t < TILES:
                    keep_v(2 * t, 4)
                    act.wait_ge(de2.deep_clamped, TILES * k + t + 1)
                    nc.scalar.activation(h_std, h_clamped, ACT.Sqrt).then_inc(de.deep_std_ready, 1)
                    keep_v(2 * t + 1, 5)
                if t in (1, 2):
                    deep_ffn_act(act, {1: "square", 2: "std"}[t], f)

            def exps(t):
                act.wait_ge(de.deep_less_max, TILES * k + t + 1)
                nc.scalar.activation(probs, probs, ACT.Exp).then_inc(de.deep_exped, 1)
            for t in range(TILES + 1):
                if t < TILES:
                    for wi in V_LATER[t]:
                        keep_v(wi, 2 + wi % 2)
                        if t == 0 and wi == V_LATER[0][1]:
                            exps(0)
                if t >= 1:
                    m = t - 1
                    for half in range(2):
                        act.wait_ge(de.deep_probs_turned, 2 * (TILES * k + m) + half + 1)
                        if m >= 1:
                            act.wait_ge(de.deep_pv_done, 2 * (TILES * k + m - 1) + half + 1)
                        nc.scalar.activation(probsT[:, half, :], bank(4 + half), ACT.Copy).then_inc(de.deep_probs_kept, 1)
                    if t < TILES:
                        exps(t)
                    for half in range(2):
                        act.wait_ge(de.deep_pv_done, 2 * (TILES * k + m) + half + 1)
                        nc.scalar.activation(oT[:, 4 * half:4 * half + 4, m * P:(m + 1) * P],
                                             bank(6 + half).rearrange("p (c t) -> p c t", t=P), ACT.Copy).then_inc(de.deep_o_kept, 1)

        def deep_dve(dve, u, n, k, b, h, f):
            W = deep_w[h]
            dve.wait_ge(g.unit_done, u - 3)
            apart(dve)
            nc.vector.tensor_copy(xs[0:64, WIN:WIN + T], z[0:64, bass.ds(b * T, T)]).then_inc(de.deep_shifted, 1)
            nc.vector.tensor_copy(xs[64:P, WIN + 1:WIN + T], z[64:P, bass.ds(b * T, T - 1)]).then_inc(de.deep_shifted, 1)
            deep_ffn_dve(dve, "start", f)
            nc.vector.tensor_tensor(tabs, w.rope64[:, :, :, :],
                                    W.scales.rearrange("p (a o) d -> p a o d", o=1).broadcast_to([P, 4, TILES, LD]),
                                    ALU.mult).then_inc(de.deep_tabs_ready, 1)
            dve.wait_ge(de.deep_tabs_ready, k + 1)
            qk = psum[:, 0:2048].rearrange("p (s h d) -> p s h d", s=2, d=LD)
            for t in range(TILES):
                i = TILES * k + t
                dve.wait_ge(de.deep_qk_squared, 2 * i + 2)
                nc.vector.tensor_reduce(h_sum, qk_sq, AX.X, ALU.add).then_inc(de2.deep_sq_summed, 1)
                dve.wait_ge(de2.deep_sq_summed, i + 1)
                nc.vector.tensor_scalar(h_clamped, h_sum, NORM_FLOOR, None, ALU.max).then_inc(de2.deep_clamped, 1)
                for s in range(2):
                    hs = slice(LHEADS * s, LHEADS * (s + 1))
                    shape = [P, LHEADS, LD]
                    swapped = qk[:, s].rearrange("p h (a e) -> p h a e", a=2)[:, :, ::-1, :]
                    sin = tabs[:, 2 * s + 1, t, :].rearrange("p (o a e) -> p o a e", o=1, a=2).broadcast_to([P, LHEADS, 2, LD // 2])
                    nc.vector.tensor_tensor(turned[:, hs, :].rearrange("p h (a e) -> p h a e", a=2), swapped, sin,
                                            ALU.mult).then_inc(de.deep_rope_parts, 1)
                    if t >= 1:
                        dve.wait_ge(de.deep_turned, 4 * i - 2 + 2 * s)
                    nc.vector.tensor_tensor(roped[:, hs, :], qk[:, s], under(tabs[:, 2 * s, t, :], shape),
                                            ALU.mult).then_inc(de.deep_rope_parts, 1)
                dve.wait_ge(de.deep_rope_parts, 4 * (i + 1))
                nc.vector.tensor_tensor(roped, roped, turned, ALU.add).then_inc(de.deep_summed, 1)
                dve.wait_ge(de.deep_std_ready, i + 1)
                nc.vector.reciprocal(h_inv, h_std).then_inc(de.deep_recip, 1)
                dve.wait_ge(de.deep_recip, i + 1)
                dve.wait_ge(de.deep_summed, i + 1)
                nc.vector.tensor_tensor(roped, roped, over(h_inv, H2), ALU.mult).then_inc(de.deep_roped, 1)
                if t in (0, 2, 3):
                    deep_ffn_dve(dve, {0: "centre", 2: "rstd", 3: "scale"}[t], f)
            for piece in (0, 1, 2, "end"):
                deep_ffn_dve(dve, piece, f)
            R = [P, LHEADS, 2 * WIN]
            flat = probs.rearrange("p a r c -> p (a r) c")
            for t in range(TILES):
                i = TILES * k + t
                mask = w.win_mask[:, 1 if t else 0, :]
                dve.wait_ge(de.deep_scores_ready, i + 1)
                if t >= 1:
                    dve.wait_ge(de.deep_probs_turned, 2 * i)
                for r in range(2):
                    nc.vector.tensor_tensor(probs[:, :, r, :], bank(r).rearrange("p (a c) -> p a c", c=64),
                                            under(mask, [P, PAIRS, 2 * WIN]), ALU.add).then_inc(de.deep_masked, 1)
                dve.wait_ge(de.deep_masked, 2 * (i + 1))
                nc.vector.tensor_reduce(row_max, flat, AX.X, ALU.max).then_inc(de.deep_max, 1)
                dve.wait_ge(de.deep_max, i + 1)
                nc.vector.tensor_tensor(flat, flat, over(row_max, R), ALU.subtract).then_inc(de.deep_less_max, 1)
                dve.wait_ge(de.deep_exped, i + 1)
                nc.vector.tensor_reduce(row_sum, flat, AX.X, ALU.add).then_inc(de.deep_row_sum, 1)
                dve.wait_ge(de.deep_row_sum, i + 1)
                nc.vector.reciprocal(row_inv, row_sum).then_inc(de.deep_row_inv, 1)
                dve.wait_ge(de.deep_row_inv, i + 1)
                nc.vector.tensor_tensor(flat, flat, over(row_inv, R), ALU.mult).then_inc(de.deep_probs_ready, 1)

        de2 = sems("deep_sq_summed deep_clamped")

        tm3 = sems("tm_const xn_zeroed")

        plan, units, norms, seen = [], 1, 0, {}
        for kind in sublayers:
            same = "dense" if kind in ("mqa", "rope") else kind
            plan.append((kind, units, norms, seen.get(same, 0), seen.get(same, 0) - seen.get("only " + kind, 0)))
            if kind == "deep":
                units, norms, many = units + NB + DEPTH * NB + 1, norms + NB + DEPTH * NB, DEPTH * NB
            elif kind == "forget":
                units, norms, many = units + 2 * NB, norms + NB, NB
            else:
                units, norms, many = units + NB, norms + NB, NB
            seen[same] = seen.get(same, 0) + many
            seen["only " + kind] = seen.get("only " + kind, 0) + many
        last_unit = units

        n_fixed = len(fixed)
        block = ctx.enter_context(nc.Block())

        def per_unit(eng, body, u, n, k, *more):
            with eng.Fori(0, NB) as b:
                body(eng, b + u, b + n, b + k, b, *more)

        def deep_pairs(eng, body, ffn, pieces, u, n, k, call):
            with eng.Fori(0, DEPTH // 2) as i:
                def count(h, b):
                    m = i * (2 * NB) + b + h * NB
                    return m + u, m + n, m + k, b, h
                for h in range(2):
                    eng.wait_ge(deep_loaded[h], i * N_DEEP + (call * DEPTH // 2 + 1) * N_DEEP)
                    body(eng, *count(h, 0), count(0, NB - 1) if h else None)
                    with eng.Fori(1, NB) as b:
                        body(eng, *count(h, b), count(h, b - 1))
                last = count(1, NB - 1)
                for piece in pieces:
                    ffn(eng, piece, last)

        N_DEEP = 16 * len(layered)

        @block.sync
        def _(sp):
            for b in range(NB):
                sp.dma_start(x[:, b * T:(b + 1) * T], d["x"][:, b * T:(b + 1) * T]).then_inc(g.x_loaded, 16)
            for name in fixed:
                dst = raw[name] if name in raw else kept[name]
                sp.dma_start(dst[tuple(slice(None) for _ in dst.shape)], d[name]).then_inc(g.weights_loaded, 16)
            calls = 0
            for kind, u, n, k, other in plan:
                if kind != "deep":
                    continue
                with sp.Fori(0, DEPTH // 2) as i:
                    for h in range(2):
                        free = u + NB + i * (2 * NB) + (h - 1) * NB
                        sp.wait_ge(g.unit_done, free)
                        for name in layered:
                            dst = deep_kept[h][name]
                            src = d[name][bass.ds(i * 2 + h, 1)]
                            if len(src.shape) == 3:
                                src = src.rearrange("l p a -> p (l a)")
                            else:
                                src = src.rearrange("l p a b -> p (l a) b")
                            sp.dma_start(dst[tuple(slice(None) for _ in dst.shape)], src).then_inc(deep_loaded[h], 16)
                calls += 1
            sp.wait_ge(g.unit_done, last_unit)
            sp.dma_start(out, x[:, :]).then_inc(g.stored, 16)
            sp.wait_ge(g.stored, 16)

        @block.gpsimd
        def _(pool):
            nc.gpsimd.memset(xn[:, 0:1], 0.0).then_inc(g.pads_zeroed, 1)
            nc.gpsimd.memset(xs[:, 0:WIN + 1], 0.0).then_inc(g.pads_zeroed, 1)
            nc.gpsimd.memset(mx[:, :, :], 0.0).then_inc(g.pads_zeroed, 1)
            nc.gpsimd.memset(deep_kT[:, :, 0:WIN], 0.0).then_inc(g.pads_zeroed, 1)
            nc.gpsimd.memset(eps[:, :], LN_EPS).then_inc(g.pads_zeroed, 1)

        PADS = 5

        def ready(eng):
            eng.wait_ge(g.x_loaded, 16 * NB)
            eng.wait_ge(g.weights_loaded, 16 * n_fixed)
            eng.wait_ge(g.pads_zeroed, PADS)

        @block.tensor
        def _(pe):
            ready(pe)
            pe.wait_ge(g.weights_scaled, 5)
            call = 0
            for kind, u, n, k, other in plan:
                if kind == "moe":
                    per_unit(pe, moe_pe, u, n, k)
                elif kind == "chan":
                    per_unit(pe, chan_pe, u, n, k)
                elif kind == "swiglu":
                    per_unit(pe, swiglu_pe, u, n, k)
                elif kind in ("mqa", "rope"):
                    per_unit(pe, dense_pe, u, n, k, kind == "mqa", other)
                elif kind == "time":
                    per_unit(pe, time_pe, u, n, k)
                elif kind == "forget":
                    per_unit(pe, forget_in_pe, u, n, k)
                    forget_out_pe(pe, u + NB)
                elif kind == "deep":
                    with pe.Fori(0, NB) as b:
                        pe.wait_ge(g.unit_done, b + u)
                        ln_pe(pe, b + n, x[:, unit(b)])
                    deep_pairs(pe, deep_pe, deep_ffn_pe, FFN_PE, u + NB, n + NB, k, call)
                    call += 1

        @block.scalar
        def _(act):
            ready(act)
            nc.scalar.activation(eu[:, :], w.tm_first[:, :], ACT.Exp).then_inc(tm3.tm_const, 1)
            nc.scalar.activation(ew[:, :], w.tm_decay[:, :], ACT.Exp).then_inc(tm3.tm_const, 1)
            act.wait_ge(tm3.tm_const, 2)
            nc.scalar.activation(ew[:, :], ew[:, :], ACT.Exp, scale=-1.0).then_inc(tm3.tm_const, 1)
            call = 0
            for kind, u, n, k, other in plan:
                if kind == "moe":
                    per_unit(act, moe_act, u, n, k)
                elif kind == "chan":
                    per_unit(act, chan_act, u, n, k)
                elif kind == "swiglu":
                    per_unit(act, swiglu_act, u, n, k)
                elif kind in ("mqa", "rope"):
                    per_unit(act, dense_act, u, n, k, kind == "mqa", other)
                elif kind == "time":
                    per_unit(act, time_act, u, n, k)
                elif kind == "forget":
                    per_unit(act, forget_in_act, u, n, k)
                elif kind == "deep":
                    with act.Fori(0, NB) as b:
                        ln_act(act, b + n)
                    deep_pairs(act, deep_act, deep_ffn_act, FFN_ACT, u + NB, n + NB, k, call)
                    call += 1

        @block.vector
        def _(dve):
            ready(dve)
            for src, dst in ((raw["sw_gate"], gate_w), (raw["sw_up"], up_w), (raw["sw_down"], down_w)):
                whole = tuple(slice(None) for _ in dst.shape)
                done = g.unit_done if dst is down_w else g.weights_scaled
                nc.vector.tensor_scalar(dst[whole], src[whole], 1.0 / 127.0, None, ALU.mult).then_inc(done, 1)
            nc.vector.tensor_copy(later_key_q[:, :], raw["later_key_q"]).then_inc(g.weights_scaled, 1)
            nc.vector.tensor_copy(later_key_k[:, :], raw["later_key_k"]).then_inc(g.weights_scaled, 1)
            nc.vector.tensor_copy(identb[:, :], w.ident[:, :]).then_inc(g.weights_scaled, 1)
            dve.wait_ge(tm3.tm_const, 3)
            call = dense_calls = 0
            for kind, u, n, k, other in plan:
                if kind == "moe":
                    per_unit(dve, moe_dve, u, n, k)
                elif kind == "chan":
                    per_unit(dve, chan_dve, u, n, k)
                elif kind == "swiglu":
                    per_unit(dve, swiglu_dve, u, n, k)
                elif kind in ("mqa", "rope"):
                    dense_lay_values(dve, dense_calls)
                    dense_calls += 1
                    per_unit(dve, dense_dve, u, n, k, kind == "mqa", other)
                elif kind == "time":
                    per_unit(dve, time_dve, u, n, k)
                elif kind == "forget":
                    per_unit(dve, forget_in_dve, u, n, k)
                    forget_out_dve(dve, u + NB)
                elif kind == "deep":
                    with dve.Fori(0, NB) as b:
                        ln_dve(dve, b + n, x[:, unit(b)], z[:, unit(b)])
                        dve.wait_ge(ln.ln_normed, b + (n + 1))
                        nc.vector.tensor_copy(h_sum[:, 0:1], rstd[:, 0:1]).then_inc(g.unit_done, 1)
                    deep_pairs(dve, deep_dve, deep_ffn_dve, FFN_DVE, u + NB, n + NB, k, call)
                    dve.wait_ge(g.unit_done, u + NB + DEPTH * NB)
                    nc.vector.memset(xn[:, 0:1], 0.0).then_inc(tm3.xn_zeroed, 1)
                    dve.wait_ge(tm3.xn_zeroed, call + 1)
                    nc.vector.scalar_tensor_tensor(x[:, :], z[:, :], 0.5, x[:, :], ALU.mult, ALU.add).then_inc(g.unit_done, 1)
                    dve.wait_ge(g.unit_done, u + NB + DEPTH * NB + 1)
                    call += 1


def constants(np):
    f = np.float32
    p = np.arange(P)
    c = {"ident": np.eye(P, dtype=f), "avg": np.full((P, P), 1.0 / P, f)}
    c["head_ones"] = (p[:, None] // HD8 == p[None, :] // HD8).astype(f)
    c["later_key_q"] = np.where(p[None, :] > p[:, None], -FAR, 0).astype(f)
    c["later_key_k"] = np.where(p[:, None] > p[None, :], -FAR, 0).astype(f)
    h = np.arange(HEADS8)
    c["row_mask"] = (p[:, None] // HD8 == h).astype(f)
    at = np.where(h < HEADS8 // 2, P // 2 + h, h - HEADS8 // 2)
    c["max_row"] = (p[:, None] == at).astype(f)
    rot = np.zeros((P, P), f)
    ev = p[::2]
    rot[ev + 1, ev] = -1.0
    rot[ev, ev + 1] = 1.0
    c["rot8"] = rot
    inv = (1.0 / f(10000.0) ** (np.arange(0, HD8, 2, dtype=f) / f(HD8))).astype(f)
    ang = np.arange(T, dtype=f)[None, :] * inv[(p % HD8) // 2][:, None]
    c["rope8"] = np.stack([np.cos(ang), np.sin(ang)], 1).astype(f)
    c["moe_order"] = np.broadcast_to(np.arange(EXPERTS, 0, -1, dtype=f), (P, EXPERTS)).copy()
    q, k = (p % WIN)[:, None], np.arange(2 * WIN)[None, :]
    band = (k >= q) & (k <= q + WIN)
    first = band & ((p[:, None] >= WIN) | (k >= WIN))
    c["win_mask"] = np.stack([np.where(first, 0, -FAR), np.where(band, 0, -FAR)], 1).astype(f)
    half = np.arange(0, LD, 2, dtype=f)
    t = np.arange(T, dtype=f)
    fr = t[:, None] * (1.0 / f(10000.0) ** (half / f(LD))).astype(f)[None, :]
    base = (half + f(0.4 * LD)) / f(1.4 * LD)
    sc = (base[None, :] ** ((t - T // 2) / f(WIN // 2))[:, None]).astype(f)
    fr, sc = np.concatenate([fr, fr], 1), np.concatenate([sc, sc], 1)
    sign = np.where(np.arange(LD) < LD // 2, -1.0, 1.0).astype(f)
    cos, sin = np.cos(fr).astype(f), np.sin(fr).astype(f) * sign
    tab = np.stack([cos * sc * 8, sin * sc * 8, cos / sc, sin / sc], 0).astype(f)
    c["rope64"] = np.ascontiguousarray(tab.reshape(4, TILES, P, LD).transpose(2, 0, 1, 3))
    return c


def laid_out(np, v):
    L = {}
    col = lambda a: a.reshape(P, 1)
    rows = lambda a: np.broadcast_to(a, (P,) + a.shape)
    L["x"] = v["L0_attn_x"].reshape(NB * T, P).T
    L["moe_wg"] = v["L0_ffn_Wg"]
    L["moe_bg"] = rows(v["L0_ffn_bg"])
    L["moe_we"] = v["L0_ffn_We"].transpose(2, 0, 1)
    L["moe_be"] = v["L0_ffn_be"]
    L["mqa_down"] = v["L0_attn_Wc_down"]
    L["mqa_q"] = v["L0_attn_Wq_up"]
    L["mqa_k"] = np.tile(v["L0_attn_Wkv_up"][:, :HD8], (1, HEADS8))
    L["mqa_v"] = np.tile(v["L0_attn_Wkv_up"][:, HD8:], (1, HEADS8))
    L["mqa_proj"] = v["L0_attn_Wc_proj"]
    for n in ("q", "k", "v", "o"):
        L["ra_w" + n] = v["L1_attn_W" + n].T
        L["fo_w" + n] = v["L2_attn_W" + n].T
        L["fo_b" + n] = col(v["L2_attn_b" + n])
        L["ra_b" + n] = rows(v["L1_attn_bv"]) if n == "v" else col(v["L1_attn_b" + n])
    L["fo_wf"] = np.repeat(v["L2_attn_Wf"].T, HD8, axis=1)
    L["fo_bf"] = col(np.repeat(v["L2_attn_bf"], HD8))
    for n in ("r", "k", "v"):
        L["cm_w" + n] = v["L1_ffn_W_" + n].T
    L["cm_mu_r"], L["cm_mu_k"] = col(v["L1_ffn_mu_r"]), col(v["L1_ffn_mu_k"])
    L["sw_gate"], L["sw_up"] = v["L2_ffn_w_gate"].T, v["L2_ffn_w_up"].T
    L["sw_down"] = v["L2_ffn_w_down"].T.reshape(HBLK, P, P).transpose(1, 0, 2)
    for n in ("k", "v", "r", "o"):
        L["tm_w" + n] = v["L3_attn_W" + n].T
    L["tm_decay"], L["tm_first"] = col(v["L3_attn_time_decay"]), col(v["L3_attn_time_first"])
    for n in ("k", "v", "r"):
        L["tm_m" + n] = col(v["L3_attn_time_mix_" + n])
    L["deep_wqkv"] = v["L3_ffn_Wqkv"]
    L["deep_wo"] = v["L3_ffn_Wo"].reshape(DEPTH, PAIRS, P, P).transpose(0, 2, 1, 3)
    L["deep_w1"] = v["L3_ffn_W1"]
    w2 = np.zeros((DEPTH, 3 * P, P), v["L3_ffn_W2"].dtype)
    w2[:, :DI] = v["L3_ffn_W2"]
    L["deep_w2"] = w2.reshape(DEPTH, 3, P, P).transpose(0, 2, 1, 3)
    b1 = np.zeros((DEPTH, 2, 3 * P), v["L3_ffn_b1"].dtype)
    b1[:, :, :DI] = v["L3_ffn_b1"].reshape(DEPTH, 2, DI)
    L["deep_vec"] = np.concatenate([v["L3_ffn_ln_g"][:, None], v["L3_ffn_ln_b"][:, None], v["L3_ffn_b2"][:, None],
                                    b1.reshape(DEPTH, 6, P)], 1).transpose(0, 2, 1)
    scales = []
    for n in ("q", "k"):
        s = v[f"L3_ffn_{n}_scale"]
        scales += [s, np.concatenate([s[:, LD // 2:], s[:, :LD // 2]], 1)]
    L["deep_scales"] = np.broadcast_to(np.stack(scales, 1)[:, None], (DEPTH, P, 4, LD))
    return L


def kernel(**inputs):
    import numpy as np
    import concourse.bacc as bacc
    from concourse.bass_utils import run_bass_kernel_spmd

    arrays = laid_out(np, {k: np.asarray(a) for k, a in inputs.items()})
    arrays.update(constants(np))
    nc = bacc.Bacc("TRN2", target_bir_lowering=False, num_devices=1)
    arrays = {k: np.ascontiguousarray(a) for k, a in arrays.items()}
    d = {k: nc.dram_tensor("in_" + k, a.shape, mybir.dt.from_np(a.dtype), kind="ExternalInput").ap()
         for k, a in arrays.items()}
    out = nc.dram_tensor("out_0_dram", (P, NB * T), F32, kind="ExternalOutput").ap()
    program(nc, d, out, SUBLAYERS)
    r = run_bass_kernel_spmd(nc, [{"in_" + k: a for k, a in arrays.items()}], core_ids=[0])
    return np.ascontiguousarray(r.results[0]["out_0_dram"].T).reshape(NB, T, P)
```
